# Optimizing a Trainium2 kernel written in Bass

```python
import numpy as np
import jax
import jax.numpy as jnp

def _softmax(x, axis=-1):
    return jax.nn.softmax(x, axis=axis)

def _gelu(x):
    return jax.nn.gelu(x, approximate=True)

def _silu(x):
    return jax.nn.silu(x)

def _sigmoid(x):
    return jax.nn.sigmoid(x)

def _layernorm(x, axis=-1, eps=1e-05):
    m = jnp.mean(x, axis=axis, keepdims=True)
    v = jnp.var(x, axis=axis, keepdims=True)
    return (x - m) / jnp.sqrt(v + eps)

def _scatter_add(tgt, idx, src, axis=0):
    return tgt.at[idx].add(src)

def _segment_sum(src, seg, n):
    return jax.ops.segment_sum(src, seg, n)
kernel_name = 'mk_adj_resnorm_d2_adj_r2_33b544'

def setup_inputs(seed: int=0):
    np.random.seed(seed)
    _w = jnp.asarray

    def _rec_inputs():
        import jax
        import jax.numpy as jnp
        _gk = jax.random.key(seed)
        x = -0.000929 + 1 * jax.random.normal(jax.random.fold_in(_gk, 1), (8192, 128), jnp.float32)
        _a = jax.random.bernoulli(jax.random.fold_in(_gk, 2), 0.000244141, (8192, 8192))
        _a = jnp.logical_or(_a, jnp.swapaxes(_a, -1, -2))
        _a = jnp.logical_or(_a, jnp.eye(8192, dtype=bool))
        _af = _a.astype(jnp.float32)
        _af = _af * jax.random.uniform(jax.random.fold_in(_gk, 3), (8192, 8192), jnp.float32, 0.05, 1)
        adj = _af
        return (x, adj)
    x, adj = _rec_inputs()

    def _L0_gnn_setup():
        import jax, jax.numpy as jnp
        import numpy as np
        N = 4096
        IN_DIM = 128
        OUT_DIM = 128
        key = jax.random.key(seed)
        k1, k2, k3, k4 = jax.random.split(key, 4)
        X = jax.random.normal(k1, (N, IN_DIM), dtype=jnp.float32)
        A = jax.random.uniform(k2, (N, N), dtype=jnp.float32)
        limit = float(np.sqrt(6.0 / (IN_DIM + OUT_DIM)))
        W = jax.random.uniform(k3, (OUT_DIM, IN_DIM), dtype=jnp.float32, minval=-limit, maxval=limit)
        b = jnp.zeros((OUT_DIM,), dtype=jnp.float32)
        return {'X': X, 'A': A, 'W': W, 'b': b}
    _L0_gnn_all = _L0_gnn_setup()
    _L0_gnn_in = {k: v for k, v in _L0_gnn_all.items() if k in ('W', 'b')}
    del _L0_gnn_all

    def _L1_gnn_setup():
        import jax, jax.numpy as jnp
        import numpy as np
        N = 8192
        F_IN = 128
        F_OUT = 128
        K = 3
        key = jax.random.key(seed)
        k1, k2, k3 = jax.random.split(key, 3)
        x = jax.random.normal(k1, (N, F_IN), dtype=jnp.float32)
        L_tilde = jax.random.normal(k2, (N, N), dtype=jnp.float32) / jnp.sqrt(jnp.float32(N))
        weight = jax.random.normal(k3, (K, F_IN, F_OUT), dtype=jnp.float32) * (1.0 / np.sqrt(F_IN))
        bias = jnp.zeros((F_OUT,), dtype=jnp.float32)
        return {'x': x, 'L_tilde': L_tilde, 'weight': weight, 'bias': bias}
    _L1_gnn_all = _L1_gnn_setup()
    _L1_gnn_in = {k: v for k, v in _L1_gnn_all.items() if k in ('weight', 'bias')}
    del _L1_gnn_all
    return {'x': x, 'adj': adj, 'L0_gnn_W': _L0_gnn_in['W'], 'L0_gnn_b': _L0_gnn_in['b'], 'L1_gnn_weight': _L1_gnn_in['weight'], 'L1_gnn_bias': _L1_gnn_in['bias']}

def reference(x, adj, L0_gnn_W, L0_gnn_b, L1_gnn_weight, L1_gnn_bias):
    import jax
    import jax.numpy as jnp

    def _L0_gnn_ref(X, A, W, b):
        import jax, jax.numpy as jnp
        import numpy as np
        N = 4096
        IN_DIM = 128
        OUT_DIM = 128
        A_hat = A + jnp.eye(A.shape[0], dtype=A.dtype)
        degree = A_hat.sum(axis=1)
        d_inv_sqrt = degree ** (-0.5)
        d_inv_sqrt = jnp.where(jnp.isinf(d_inv_sqrt), 0.0, d_inv_sqrt)
        A_norm = d_inv_sqrt[:, None] * A_hat * d_inv_sqrt[None, :]
        h = A_norm @ X
        return h @ W.T + b

    def _L1_gnn_ref(x, L_tilde, weight, bias):
        import jax, jax.numpy as jnp
        import numpy as np
        N = 8192
        F_IN = 128
        F_OUT = 128
        K = 3
        T_prev = x
        T_curr = L_tilde @ x
        out = T_prev @ weight[0]
        if K > 1:
            out = out + T_curr @ weight[1]
        for k in range(2, K):
            T_next = 2.0 * (L_tilde @ T_curr) - T_prev
            out = out + T_next @ weight[k]
            T_prev, T_curr = (T_curr, T_next)
        return out + bias
    x = _layernorm(x + _L0_gnn_ref(x, adj, L0_gnn_W, L0_gnn_b), axis=-1)
    x = _layernorm(x + _L1_gnn_ref(x, adj, L1_gnn_weight, L1_gnn_bias), axis=-1)
    return x

_drawn_inputs = setup_inputs


def setup_inputs(seed=0):
    import zlib

    import numpy as np

    out = dict(_drawn_inputs(seed))
    spreads = {'L0_gnn_b': (0.0, 0.1), 'L1_gnn_bias': (0.0, 0.335)}
    factors = {}
    for name, (base, spread) in spreads.items():
        noise = np.random.default_rng([zlib.crc32(name.encode()), seed]).standard_normal(out[name].shape)
        drawn = base * np.exp(spread * noise) if base else spread * noise
        out[name] = jnp.asarray(drawn.astype(out[name].dtype))
    for name, factor in factors.items():
        out[name] = (out[name] * factor).astype(out[name].dtype)
    return out
```

```python
from contextlib import ExitStack

import concourse.bass as bass
from concourse import mybir

ALU = mybir.AluOpType
ACT = mybir.ActivationFunctionType
AX_X = mybir.AxisListType.X
F32 = mybir.dt.float32
BF16 = mybir.dt.bfloat16

P = 128
Q = 32
NQ = P // Q
BLK = 1024
HALF = 512
CH = BLK // P
COLS_Q = BLK // NQ
GR = HALF // Q
TILE = HALF * BLK // P
STRIPS = HALF // P
DMAS = 4
LN_EPS = 1e-5


def tri(n):
    return n * (n + 1) // 2


def build(nc, x, adj, w0, b0, w1, b1, out):
    N, D = x.shape
    NB = N // BLK
    assert D == P and adj.shape[0] == N and NB >= 4

    LOWER = tri(NB)
    STRICT = tri(NB - 1)
    LOAD2, LOAD3, LOAD4 = NB * NB, NB * NB + STRICT, NB * NB + STRICT + LOWER
    A2, A3, A4 = LOWER, LOWER + STRICT, LOWER + 2 * STRICT
    B3 = STRICT

    def a_1(i, j): return tri(i) + j
    def load_2(k, m): return LOAD2 + tri(k) + m
    def a_2(k, m): return A2 + tri(k) + m
    def b_2(k, m): return tri(k) + m
    def load_3(i, j): return LOAD3 + tri(i) + j
    def a_3(i, j): return A3 + tri(i - 1) + j
    def b_3(i, j): return B3 + tri(i) + j
    def load_4(r, m): return LOAD4 + tri(r) + m
    def a_4(r, m): return A4 + tri(r) + m

    def turned_2(k, m): return A2 + tri(k) + m
    def turned_3(i, j): return A2 + STRICT + tri(i) + j
    def turned_4(r, m): return A2 + STRICT + LOWER + tri(r) + m

    with ExitStack() as ctx:
        def sb(name, shape, dt=F32):
            return ctx.enter_context(nc.sbuf_tensor(name, shape, dt))

        def ps(name, shape):
            return ctx.enter_context(nc.psum_tensor(name, shape, F32))

        def sem(name):
            return ctx.enter_context(nc.semaphore(name))

        nat = [sb(f"nat{h}", [P, TILE]) for h in range(2)]
        at = [sb(f"at{h}", [P, TILE]) for h in range(2)]
        dx_t = sb("dx_t", [P, NB * BLK])
        x1 = sb("x1", [P, NB * BLK])
        part = sb("part", [P, NB * BLK])
        wa = sb("wa", [P, BLK])
        wb = sb("wb", [P, BLK])
        xrow = sb("xrow", [P, BLK])
        trow = sb("trow", [P, BLK])
        p0 = sb("p0", [P, BLK])
        p1 = sb("p1", [P, BLK])
        p2 = sb("p2", [P, BLK])
        z = sb("z", [P, BLK])
        y = sb("y", [P, BLK])
        w0n = sb("w0n", [P, D])
        w0t = sb("w0t", [P, D])
        cheb = sb("cheb", [P, 3 * D])
        bias0 = sb("bias0", [P, D])
        bias1 = sb("bias1", [P, D])
        ident = sb("ident", [P, P])
        same_r = sb("same_r", [P, P])
        same_q = [sb(f"same_q{q}", [P, P]) for q in range(NQ)]
        zero_w = sb("zero_w", [P, P], BF16)
        zero_m = sb("zero_m", [P, HALF], BF16)
        low_sum = sb("low_sum", [P, 2 * GR * NB])
        up_sum = sb("up_sum", [P, 2 * STRIPS * NB])
        zero_s = sb("zero_s", [P, 2 * STRIPS])
        low1 = sb("low1", [P, 2 * GR])
        up1 = sb("up1", [P, 2 * STRIPS])
        dcol = sb("dcol", [P, NB * CH])
        deg = sb("deg", [P, CH])
        is0 = sb("is0", [P, CH])
        safe = sb("safe", [P, CH])
        root = sb("root", [P, CH])
        mean = sb("mean", [P, CH])
        var = sb("var", [P, CH])
        rstd = sb("rstd", [P, CH])
        neg_half = sb("neg_half", [P, CH])

        acc_a = ps("acc_a", [P, 2, HALF])
        acc_b = ps("acc_b", [P, 2, HALF])
        s0 = ps("s0", [P, BLK])
        s1 = ps("s1", [P, BLK])

        const_in = sem("const_in")
        pool_const = sem("pool_const")
        dve_const = sem("dve_const")
        w0_turned = sem("w0_turned")
        tile_in = [sem(f"tile_in{h}") for h in range(2)]
        summed = [sem(f"summed{h}") for h in range(2)]
        turned = [sem(f"turned{h}") for h in range(2)]
        wa_set = sem("wa_set")
        wb_set = sem("wb_set")
        wa_low_used = sem("wa_low_used")
        wb_low_used = sem("wb_low_used")
        a_done = [sem(f"a_done{h}") for h in range(2)]
        b_done = [sem(f"b_done{h}") for h in range(2)]
        a_taken = [sem(f"a_taken{h}") for h in range(2)]
        b_taken = [sem(f"b_taken{h}") for h in range(2)]
        xrow_in = sem("xrow_in")
        xrow_read = sem("xrow_read")
        up_zeroed = sem("up_zeroed")
        sums_set = sem("sums_set")
        deg_ps = sem("deg_ps")
        safe_set = sem("safe_set")
        root_set = sem("root_set")
        dx_set = sem("dx_set")
        p0_set = sem("p0_set")
        part_zero = sem("part_zero")
        z_ps = sem("z_ps")
        s0_read = sem("s0_read")
        var_set = sem("var_set")
        rstd_set = sem("rstd_set")
        x1_set = sem("x1_set")
        t_ps = sem("t_ps")
        t_set = sem("t_set")
        rows_set = sem("rows_set")
        rows_ps = sem("rows_ps")
        p12_set = sem("p12_set")
        u_read = sem("u_read")
        t2_set = sem("t2_set")
        out_ps = sem("out_ps")
        y_set = sem("y_set")
        y_out = sem("y_out")
        steps1 = sem("steps1")
        steps2 = sem("steps2")
        steps4 = sem("steps4")
        own_wait = sem("own_wait")
        DVE_CONST = 4 + NQ + 2 * NQ + 1

        def alone(wait):
            wait.then_inc(own_wait, 1)

        def blockof(t, i):
            return t[:, bass.ds(i * BLK, BLK)]

        def halfof(t, i, h):
            return t[:, bass.ds(i * BLK + h * HALF, HALF)]

        def per_chunk(t):
            return t.rearrange("p (b d) -> p b d", b=CH)

        def over_features(t):
            return t.unsqueeze(2).broadcast_to([P, CH, D])

        def over_chunks(t):
            return t.unsqueeze(1).broadcast_to([P, CH, D])

        def packed(t, h):
            return t[:].rearrange("p (b a c) -> p a b c", b=CH, a=NQ)[:, 2 * h:2 * h + 2]

        def in_order(t):
            return t.rearrange("p (a b c) -> p a b c", a=2, b=CH)

        def node_rows(t, i, a):
            return t[bass.ds(i * BLK + a * COLS_Q, COLS_Q), :].rearrange("(b c) d -> c b d", c=Q)

        block = ctx.enter_context(nc.Block())

        @block.sync
        def _(sp):
            sp.dma_start(w0n[:], w0).then_inc(const_in, 16)
            sp.dma_start(cheb[:].rearrange("p (k o) -> p k o", k=3), w1.rearrange("k d o -> d k o")).then_inc(const_in, 16)
            sp.dma_start(bias0[:], b0.partition_broadcast(P)).then_inc(const_in, 16)
            sp.dma_start(bias1[:], b1.partition_broadcast(P)).then_inc(const_in, 16)

            def square(i, j, squares, blocks=NB * NB):
                for h in range(2):
                    alone(sp.wait_ge(turned[h], squares))
                    alone(sp.wait_ge(summed[h], blocks))
                    for a in range(NQ):
                        src = adj[bass.ds(i * BLK + h * HALF, HALF), bass.ds(j * BLK + a * COLS_Q, COLS_Q)]
                        dst = nat[h][Q * a:Q * a + Q, :].rearrange("r (g c) -> r g c", g=GR)
                        sp.dma_start(dst, src.rearrange("(g r) c -> r g c", r=Q)).then_inc(tile_in[h], 16)

            def strips(i, j, squares, blocks):
                for h in range(2):
                    alone(sp.wait_ge(turned[h], squares))
                    alone(sp.wait_ge(summed[h], blocks))
                    for s in range(STRIPS):
                        src = adj[bass.ds(i * BLK + h * HALF + s * P, P), bass.ds(j * BLK, BLK)]
                        sp.dma_start(nat[h][:, s * BLK:(s + 1) * BLK], src).then_inc(tile_in[h], 16)

            def row_1(i, lower, upper, last_upper=False):
                if lower:
                    with sp.Fori(0, i) as j:
                        square(i, j, a_1(i, j), NB * i + j)
                if upper:
                    strips(i, i + 1, a_1(i, i), NB * i + i)
                if upper and not last_upper:
                    with sp.Fori(i + 2, NB) as j:
                        strips(i, j, a_1(i, i), NB * i + j - 1)
                square(i, i, a_1(i, i), NB * i + NB - 1)

            row_1(0, False, True)
            with sp.Fori(1, NB - 2) as i:
                row_1(i, True, True)
            row_1(NB - 2, True, True, last_upper=True)
            row_1(NB - 1, True, False)
            with sp.Fori(0, NB - 1) as k:
                with sp.Fori(0, k + 1) as m:
                    square(NB - 2 - k, NB - 1 - m, turned_2(k, m))
            with sp.Fori(0, NB) as i:
                with sp.Fori(0, i + 1) as j:
                    square(i, j, turned_3(i, j))
            with sp.Fori(0, NB) as r:
                with sp.Fori(0, r + 1) as m:
                    square(NB - 1 - r, NB - 1 - m, turned_4(r, m))

        @block.gpsimd
        def _(pool):
            nc.gpsimd.memset(ident[:], 0.0).then_inc(pool_const, 1)
            nc.gpsimd.memset(neg_half[:], -0.5).then_inc(pool_const, 1)
            pool.wait_ge(pool_const, 2)
            nc.gpsimd.affine_select(out=ident[:], in_=ident[:], compare_op=ALU.not_equal, fill=1.0, base=0,
                                    pattern=[[-1, P]], channel_multiplier=1).then_inc(pool_const, 1)

            def load_x(i):
                for a in range(NQ):
                    dst = xrow[Q * a:Q * a + Q, :].rearrange("c (b d) -> c b d", b=CH)
                    pool.dma_start(dst, node_rows(x, i, a)).then_inc(xrow_in, 16)

            load_x(0)
            pool.wait_ge(safe_set, 1)
            nc.gpsimd.tensor_tensor(root[:], safe[:], neg_half[:], ALU.pow).then_inc(root_set, 1)
            with pool.Fori(1, NB) as i:
                alone(pool.wait_ge(dx_set, i))
                load_x(i)
                pool.wait_ge(safe_set, i + 1)
                nc.gpsimd.tensor_tensor(root[:], safe[:], neg_half[:], ALU.pow).then_inc(root_set, 1)
            pool.wait_ge(dx_set, NB)
            load_x(NB - 1)
            pool.wait_ge(var_set, 1)
            nc.gpsimd.tensor_tensor(rstd[:], var[:], neg_half[:], ALU.pow).then_inc(rstd_set, 1)
            with pool.Fori(1, NB) as r:
                alone(pool.wait_ge(xrow_read, r))
                load_x(NB - 1 - r)
                pool.wait_ge(var_set, r + 1)
                nc.gpsimd.tensor_tensor(rstd[:], var[:], neg_half[:], ALU.pow).then_inc(rstd_set, 1)
            with pool.Fori(0, NB) as r:
                pool.wait_ge(var_set, NB + r + 1)
                nc.gpsimd.tensor_tensor(rstd[:], var[:], neg_half[:], ALU.pow).then_inc(rstd_set, 1)
                alone(pool.wait_ge(y_set, r + 1))
                for a in range(NQ):
                    src = y[Q * a:Q * a + Q, :].rearrange("c (b d) -> c b d", b=CH)
                    pool.dma_start(node_rows(out, NB - 1 - r, a), src).then_inc(y_out, 16)
            pool.wait_ge(y_out, 16 * NQ * NB)

        @block.scalar
        def _(act):
            def copy(dst, src):
                return nc.scalar.activation(dst, src, ACT.Copy)

            def stage_a(j, a, first=False):
                if not first:
                    act.wait_ge(wa_low_used, a)
                copy(wa[:, 0:HALF], halfof(dx_t, j, 0)).then_inc(wa_set, 1)
                if not first:
                    act.wait_ge(a_done[1], a)
                copy(wa[:, HALF:BLK], halfof(dx_t, j, 1)).then_inc(wa_set, 1)

            def stage_b(j, b, first=False):
                if not first:
                    act.wait_ge(wb_low_used, b)
                copy(wb[:, 0:HALF], halfof(x1, j, 0)).then_inc(wb_set, 1)
                if not first:
                    act.wait_ge(b_done[1], b)
                copy(wb[:, HALF:BLK], halfof(x1, j, 1)).then_inc(wb_set, 1)

            def row_1(i, lower, upper):
                if lower:
                    with act.Fori(0, i) as j:
                        stage_a(j, a_1(i, j))
                act.wait_ge(sums_set, 2 * i)
                ups = up_sum[:].rearrange("p (s j) -> p s j", j=NB)
                copy(ups[:, :, bass.ds(i, 1)], zero_s[:].unsqueeze(2)).then_inc(up_zeroed, 1)
                if upper:
                    with act.Fori(i + 1, NB) as j:
                        for h in range(2):
                            act.wait_ge(tile_in[h], 16 * DMAS * (NB * i + j))
                            for s in range(STRIPS):
                                strip = nat[h][:, s * BLK:(s + 1) * BLK]
                                last = nc.scalar.activation(strip, strip, ACT.Copy,
                                                            accum_out=ups[:, STRIPS * h + s, bass.ds(j, 1)])
                            last.then_inc(summed[h], 1)
                act.wait_ge(dx_set, i + 1)
                stage_a(i, a_1(i, i), first=not lower)
                for h in range(2):
                    act.wait_ge(a_done[h], a_1(i, i) + 1)
                    copy(halfof(part, i, h), acc_a[:, h]).then_inc(a_taken[h], 1)

            act.wait_ge(dve_const, DVE_CONST)
            row_1(0, False, True)
            with act.Fori(1, NB - 1) as i:
                row_1(i, True, True)
            row_1(NB - 1, True, False)

            def take_b(k, h):
                act.wait_ge(p0_set, 2 * (k + 2))
                act.wait_ge(b_done[h], tri(k + 1))
                copy(halfof(part, NB - 2 - k, h), acc_b[:, h]).then_inc(b_taken[h], 1)

            stage_a(NB - 1, a_2(0, 0))
            act.wait_ge(x1_set, 1)
            stage_b(NB - 1, 0, first=True)
            with act.Fori(1, NB - 1) as k:
                take_b(k - 1, 0)
                stage_a(NB - 1, a_2(k, 0))
                stage_b(NB - 1, b_2(k, 0))
                take_b(k - 1, 1)
                with act.Fori(1, k + 1) as m:
                    stage_a(NB - 1 - m, a_2(k, m))
                    act.wait_ge(x1_set, m + 1)
                    stage_b(NB - 1 - m, b_2(k, m))
            take_b(NB - 2, 0)
            take_b(NB - 2, 1)

            def take_t(i):
                act.wait_ge(t_ps, i + 1)
                copy(blockof(dx_t, i), s0[:]).then_inc(t_set, 1)
                act.wait_ge(t_set, i + 1)

            def row_3(i, middle):
                stage_b(0, b_3(i, 0))
                take_t(i - 1)
                stage_a(0, a_3(i, 0))
                if middle:
                    with act.Fori(1, i) as j:
                        stage_b(j, b_3(i, j))
                        stage_a(j, a_3(i, j))
                stage_b(i, b_3(i, i))
                for h in range(2):
                    act.wait_ge(a_done[h], a_3(i, i))
                    act.wait_ge(p0_set, 2 * NB + 2 * i + h + 1)
                    copy(halfof(part, i, h), acc_a[:, h]).then_inc(a_taken[h], 1)

            act.wait_ge(x1_set, NB)
            stage_b(0, b_3(0, 0))
            row_3(1, False)
            with act.Fori(2, NB) as i:
                row_3(i, True)
            take_t(NB - 1)

            def stage_rows(r):
                act.wait_ge(rows_ps, 2 * r)
                copy(xrow[:], blockof(x1, NB - 1 - r)).then_inc(rows_set, 1)
                copy(trow[:], blockof(dx_t, NB - 1 - r)).then_inc(rows_set, 1)

            def take_rows(r):
                act.wait_ge(out_ps, r)
                act.wait_ge(rows_ps, 2 * r + 1)
                copy(p1[:], s0[:]).then_inc(p12_set, 1)
                act.wait_ge(rows_ps, 2 * r + 2)
                copy(p2[:], s1[:]).then_inc(p12_set, 1)

            act.wait_ge(xrow_read, NB)
            stage_a(NB - 1, a_4(0, 0))
            stage_rows(0)
            take_rows(0)
            with act.Fori(1, NB) as r:
                stage_a(NB - 1, a_4(r, 0))
                stage_rows(r)
                with act.Fori(1, r + 1) as m:
                    stage_a(NB - 1 - m, a_4(r, m))
                take_rows(r)

        @block.vector
        def _(dve):
            nc.vector.memset(zero_s[:], 0.0).then_inc(dve_const, 1)
            nc.vector.memset(zero_w[:], 0.0).then_inc(dve_const, 1)
            nc.vector.memset(zero_m[:], 0.0).then_inc(dve_const, 1)
            nc.vector.memset(low_sum[:], 0.0).then_inc(dve_const, 1)
            for q in range(NQ):
                nc.vector.memset(same_q[q][:], 0.0).then_inc(dve_const, 1)
            dve.wait_ge(pool_const, 3)
            dve.wait_ge(dve_const, 4 + NQ)
            for q in range(NQ):
                rows = slice(Q * q, Q * q + Q)
                corner = ident[rows, Q * q:Q * q + Q].unsqueeze(1).broadcast_to([Q, NQ, Q])
                nc.vector.tensor_copy(same_r[rows, :].rearrange("p (a c) -> p a c", a=NQ), corner).then_inc(dve_const, 1)
                nc.vector.tensor_copy(same_q[q][rows, :].rearrange("p (a c) -> p a c", a=NQ), corner).then_inc(dve_const, 1)
            dve.wait_ge(w0_turned, 1)
            nc.vector.tensor_copy(w0t[:], s1[:, 0:D]).then_inc(dve_const, 1)

            def own_order(signal, start):
                count = [0]

                def step(ins):
                    count[0] += 1
                    ins.then_inc(signal, 1)
                    dve.wait_ge(signal, start + count[0])
                return step

            def turn(h, a, b=None):
                dve.wait_ge(a_done[h], a)
                if b is not None:
                    dve.wait_ge(b_done[h], b)
                src = nat[h][:].rearrange("p (g b c) -> p g b c", g=GR, b=CH)
                dst = at[h][:].rearrange("p (b g r) -> p g b r", b=CH, g=GR)
                nc.vector.transpose(dst, src).then_inc(turned[h], 1)

            def arrived(h, blocks):
                dve.wait_ge(tile_in[h], 16 * DMAS * (blocks + 1))

            STEPS1 = NQ + 3

            def turn_and_sum(i, j, place, h):
                arrived(h, NB * i + place)
                turn(h, a_1(i, j))
                sums = low_sum[:].rearrange("p (g j) -> p g j", j=NB)[:, GR * h:GR * h + GR, bass.ds(j, 1)]
                nc.vector.tensor_reduce(sums, nat[h][:].rearrange("p (g o c) -> p g o c", g=GR, o=1), AX_X,
                                        ALU.add).then_inc(summed[h], 1)

            def row_1(i, lower):
                step = own_order(steps1, STEPS1 * i)
                if lower:
                    with dve.Fori(0, i) as j:
                        for h in range(2):
                            turn_and_sum(i, j, j, h)
                for h in range(2):
                    turn_and_sum(i, i, NB - 1, h)
                dve.wait_ge(deg_ps, i)
                for h in range(2):
                    dve.wait_ge(summed[h], NB * i + NB)
                nc.vector.tensor_reduce(low1[:], low_sum[:].rearrange("p (g j) -> p g j", j=NB), AX_X,
                                        ALU.add).then_inc(sums_set, 1)
                dve.wait_ge(up_zeroed, i + 1)
                nc.vector.tensor_reduce(up1[:], up_sum[:].rearrange("p (s j) -> p s j", j=NB), AX_X,
                                        ALU.add).then_inc(sums_set, 1)
                dve.wait_ge(deg_ps, i + 1)
                for a in range(NQ):
                    rows = slice(Q * a, Q * a + Q)
                    step(nc.vector.tensor_scalar(deg[rows, :], s1[rows, CH * a:CH * a + CH], 1.0, None, ALU.add))
                step(nc.vector.tensor_scalar(is0[:], deg[:], 0.0, None, ALU.is_equal))
                nc.vector.tensor_tensor(safe[:], deg[:], is0[:], ALU.add).then_inc(safe_set, 1)
                dve.wait_ge(safe_set, i + 1)
                step(nc.vector.tensor_scalar(is0[:], is0[:], -1.0, 1.0, ALU.mult, ALU.add))
                dve.wait_ge(root_set, i + 1)
                d_i = dcol[:, bass.ds(i * CH, CH)]
                step(nc.vector.tensor_tensor(d_i, root[:], is0[:], ALU.mult))
                dve.wait_ge(xrow_in, 16 * NQ * (i + 1))
                nc.vector.tensor_tensor(per_chunk(blockof(dx_t, i)), per_chunk(xrow[:]), over_features(d_i),
                                        ALU.mult).then_inc(dx_set, 1)

            row_1(0, False)
            with dve.Fori(1, NB) as i:
                row_1(i, True)

            def norm(step, rows, dst, dst_free, signal):
                step(nc.vector.tensor_reduce(mean[:], per_chunk(z[:]), AX_X, ALU.add))
                step(nc.vector.tensor_scalar(mean[:], mean[:], 1.0 / D, None, ALU.mult))
                step(nc.vector.tensor_tensor(per_chunk(z[:]), per_chunk(z[:]), over_features(mean[:]), ALU.subtract))
                dst_free()
                step(nc.vector.tensor_tensor(y[:], z[:], z[:], ALU.mult))
                step(nc.vector.tensor_reduce(var[:], per_chunk(y[:]), AX_X, ALU.add))
                nc.vector.tensor_scalar(var[:], var[:], 1.0 / D, LN_EPS, ALU.mult, ALU.add).then_inc(var_set, 1)
                dve.wait_ge(rstd_set, rows + 1)
                nc.vector.tensor_tensor(per_chunk(dst), per_chunk(z[:]), over_features(rstd[:]),
                                        ALU.mult).then_inc(signal, 1)

            STEPS2 = 6

            def h_half(r, h):
                dve.wait_ge(z_ps, r)
                alone(dve.wait_ge(a_done[h], A2 + tri(r)))
                nc.vector.tensor_tensor(packed(p0, h), in_order(acc_a[:, h]), in_order(halfof(part, NB - 1 - r, h)),
                                        ALU.add).then_inc(p0_set, 1)

            def norm_0(r):
                step = own_order(steps2, STEPS2 * r)
                i = NB - 1 - r
                dve.wait_ge(z_ps, r + 1)
                nc.vector.tensor_tensor(per_chunk(z[:]), per_chunk(s0[:]), over_features(dcol[:, bass.ds(i * CH, CH)]),
                                        ALU.mult).then_inc(s0_read, 1)
                dve.wait_ge(s0_read, r + 1)
                dve.wait_ge(xrow_in, 16 * NQ * (NB + r + 1))
                nc.vector.tensor_tensor(z[:], z[:], xrow[:], ALU.add).then_inc(xrow_read, 1)
                dve.wait_ge(xrow_read, r + 1)
                step(nc.vector.tensor_tensor(per_chunk(z[:]), per_chunk(z[:]), over_chunks(bias0[:]), ALU.add))
                norm(step, r, blockof(x1, i), lambda: None, x1_set)

            for h in range(2):
                dve.wait_ge(a_taken[h], NB)
                nc.vector.tensor_copy(packed(p0, h), in_order(halfof(part, NB - 1, h))).then_inc(p0_set, 1)
            dve.wait_ge(p0_set, 2)
            nc.vector.memset(blockof(part, NB - 1), 0.0).then_inc(part_zero, 1)
            norm_0(0)
            for h in range(2):
                arrived(h, load_2(0, 0))
                turn(h, a_2(0, 0))
            with dve.Fori(1, NB - 1) as k:
                arrived(0, load_2(k, 0))
                h_half(k, 0)
                turn(0, a_2(k, 0), b_2(k, 0))
                h_half(k, 1)
                arrived(1, load_2(k, 0))
                turn(1, a_2(k, 0), b_2(k, 0))
                norm_0(k)
                with dve.Fori(1, k + 1) as m:
                    for h in range(2):
                        arrived(h, load_2(k, m))
                        turn(h, a_2(k, m), b_2(k, m))
            h_half(NB - 1, 0)
            h_half(NB - 1, 1)
            norm_0(NB - 1)

            def t_half(i, h):
                dve.wait_ge(z_ps, NB)
                dve.wait_ge(t_ps, i)
                dve.wait_ge(b_done[h], b_3(i, i) + 1)
                nc.vector.tensor_tensor(packed(p0, h), in_order(acc_b[:, h]), in_order(halfof(part, i, h)),
                                        ALU.add).then_inc(p0_set, 1)

            dve.wait_ge(part_zero, 1)
            for h in range(2):
                dve.wait_ge(b_taken[h], NB - 1)
                arrived(h, load_3(0, 0))
                turn(h, a_3(0, 0), b_3(0, 0))

            def row_3(i):
                t_half(i - 1, 0)
                arrived(0, load_3(i, 0))
                turn(0, a_3(i, 0), b_3(i, 0))
                t_half(i - 1, 1)
                arrived(1, load_3(i, 0))
                turn(1, a_3(i, 0), b_3(i, 0))
                with dve.Fori(1, i + 1) as j:
                    for h in range(2):
                        arrived(h, load_3(i, j))
                        turn(h, a_3(i, j), b_3(i, j))

            row_3(1)
            dve.wait_ge(p0_set, 2 * NB + 2)
            nc.vector.memset(blockof(part, 0), 0.0).then_inc(part_zero, 1)
            with dve.Fori(2, NB) as i:
                row_3(i)
            t_half(NB - 1, 0)
            t_half(NB - 1, 1)

            STEPS4 = 6

            def u_half(r, h):
                dve.wait_ge(out_ps, r)
                alone(dve.wait_ge(a_done[h], A4 + tri(r + 1)))
                nc.vector.tensor_tensor(packed(p0, h), in_order(acc_a[:, h]), in_order(halfof(part, NB - 1 - r, h)),
                                        ALU.add).then_inc(u_read, 1)

            def t2(r):
                dve.wait_ge(u_read, 2 * r + 2)
                dve.wait_ge(p12_set, 2 * r + 1)
                nc.vector.scalar_tensor_tensor(out=p0[:], in0=p0[:], scalar=2.0, in1=p1[:], op0=ALU.mult,
                                               op1=ALU.subtract).then_inc(t2_set, 1)

            def norm_1(r):
                step = own_order(steps4, STEPS4 * r)
                dve.wait_ge(out_ps, r + 1)
                nc.vector.tensor_tensor(z[:], s0[:], blockof(x1, NB - 1 - r), ALU.add).then_inc(s0_read, 1)
                dve.wait_ge(s0_read, NB + r + 1)
                step(nc.vector.tensor_tensor(per_chunk(z[:]), per_chunk(z[:]), over_chunks(bias1[:]), ALU.add))
                norm(step, NB + r, y[:], lambda: dve.wait_ge(y_out, 16 * NQ * r), y_set)

            dve.wait_ge(t_ps, NB)
            dve.wait_ge(part_zero, 2)
            for h in range(2):
                dve.wait_ge(a_taken[h], 2 * NB - 1)
                arrived(h, load_4(0, 0))
                turn(h, a_4(0, 0), B3 + LOWER)

            def row_4(r):
                u_half(r - 1, 0)
                arrived(0, load_4(r, 0))
                turn(0, a_4(r, 0))
                u_half(r - 1, 1)
                t2(r - 1)
                arrived(1, load_4(r, 0))
                turn(1, a_4(r, 0))
                norm_1(r - 1)
                with dve.Fori(1, r + 1) as m:
                    for h in range(2):
                        arrived(h, load_4(r, m))
                        turn(h, a_4(r, m))

            row_4(1)
            with dve.Fori(2, NB) as r:
                row_4(r)
            u_half(NB - 1, 0)
            u_half(NB - 1, 1)
            t2(NB - 1)
            norm_1(NB - 1)

        @block.tensor
        def _(pe):
            def chunk(t, b):
                return t[:, b * P:(b + 1) * P]

            def clear(acc, h):
                pe.matmul(acc[:, h], zero_w[:], zero_m[:], start=True, stop=False, skip_group_check=True)

            def products(acc, w, h, w_set, low_used, done, blocks, add_ident=False):
                for b in range(CH):
                    if h == 0 and b % (CH // 2) == 0:
                        pe.wait_ge(w_set, 2 * blocks + 1 + b // (CH // 2))
                    if add_ident:
                        to = acc[:, h].rearrange("p (a b c) -> p a b c", a=2, b=CH)[:, :, b]
                        eye = ident[:, 2 * Q * h:2 * Q * (h + 1)].rearrange("p (a c) -> p a c", a=2)
                        pe.matmul(to, chunk(w, b), eye, start=False, stop=False, skip_group_check=True)
                    mm = pe.matmul(acc[:, h], chunk(w, b), at[h][:, b * HALF:(b + 1) * HALF], start=False,
                                   stop=(b == CH - 1), skip_group_check=True)
                    if h == 1 and b == CH // 2 - 1:
                        mm.then_inc(low_used, 1)
                mm.then_inc(done[h], 1)

            def into_a(h, blocks, add_ident=False):
                products(acc_a, wa, h, wa_set, wa_low_used, a_done, blocks, add_ident)

            def into_b(h, blocks):
                products(acc_b, wb, h, wb_set, wb_low_used, b_done, blocks)

            pe.wait_ge(const_in, 16 * 4)
            pe.wait_ge(pool_const, 3)
            pe.transpose(s1[:, 0:D], w0n[:], ident[:]).then_inc(w0_turned, 1)
            pe.wait_ge(dve_const, DVE_CONST)

            def row_1(i, lower):
                for h in range(2):
                    pe.wait_ge(a_taken[h], i)
                    clear(acc_a, h)
                if lower:
                    with pe.Fori(0, i) as j:
                        for h in range(2):
                            pe.wait_ge(turned[h], a_1(i, j) + 1)
                            into_a(h, a_1(i, j))
                pe.wait_ge(sums_set, 2 * i + 2)
                pe.wait_ge(safe_set, i)
                pe.matmul(s1[:, 0:2 * GR], same_r[:], low1[:], start=True, stop=False, skip_group_check=True)
                for q in range(NQ):
                    to = s1[:, 0:2 * GR].rearrange("p (s q) -> p q s", q=NQ)[:, q]
                    mm = pe.matmul(to, same_q[q][:], up1[:], start=False, stop=(q == NQ - 1), skip_group_check=True)
                mm.then_inc(deg_ps, 1)
                for h in range(2):
                    pe.wait_ge(turned[h], a_1(i, i) + 1)
                    into_a(h, a_1(i, i), add_ident=True)

            row_1(0, False)
            with pe.Fori(1, NB) as i:
                row_1(i, True)

            def z_row(r):
                pe.wait_ge(p0_set, 2 * r + 2)
                pe.wait_ge(s0_read, r)
                for b in range(CH):
                    mm = pe.matmul(chunk(s0, b), chunk(p0, b), w0t[:], start=True, stop=True, skip_group_check=True)
                mm.then_inc(z_ps, 1)

            def first_2(k):
                for h in range(2):
                    pe.wait_ge(turned[h], turned_2(k, 0) + 1)
                    if isinstance(k, int):
                        pe.wait_ge(a_taken[h], NB)
                    else:
                        pe.wait_ge(p0_set, 2 * k + h + 1)
                    clear(acc_a, h)
                    into_a(h, a_2(k, 0))
                    pe.wait_ge(b_taken[h], k)
                    clear(acc_b, h)
                    into_b(h, b_2(k, 0))

            z_row(0)
            first_2(0)
            with pe.Fori(1, NB - 1) as k:
                z_row(k)
                first_2(k)
                with pe.Fori(1, k + 1) as m:
                    for h in range(2):
                        pe.wait_ge(turned[h], turned_2(k, m) + 1)
                        into_a(h, a_2(k, m))
                        into_b(h, b_2(k, m))
            z_row(NB - 1)

            def t_row(i):
                pe.wait_ge(p0_set, 2 * NB + 2 * i + 2)
                pe.wait_ge(s0_read, NB)
                pe.wait_ge(t_set, i)
                for b in range(CH):
                    mm = pe.transpose(chunk(s0, b), chunk(p0, b), ident[:])
                mm.then_inc(t_ps, 1)

            for h in range(2):
                pe.wait_ge(turned[h], turned_3(0, 0) + 1)
                pe.wait_ge(b_taken[h], NB - 1)
                clear(acc_b, h)
                into_b(h, b_3(0, 0))

            def row_3(i, middle):
                for h in range(2):
                    pe.wait_ge(turned[h], turned_3(i, 0) + 1)
                    pe.wait_ge(p0_set, 2 * NB + 2 * i - 1 + h)
                    clear(acc_b, h)
                    into_b(h, b_3(i, 0))
                    if h == 0:
                        t_row(i - 1)
                    pe.wait_ge(a_taken[h], NB + i - 1)
                    clear(acc_a, h)
                    into_a(h, a_3(i, 0))
                if middle:
                    with pe.Fori(1, i) as j:
                        for h in range(2):
                            pe.wait_ge(turned[h], turned_3(i, j) + 1)
                            into_b(h, b_3(i, j))
                            into_a(h, a_3(i, j))
                for h in range(2):
                    pe.wait_ge(turned[h], turned_3(i, i) + 1)
                    into_b(h, b_3(i, i))

            row_3(1, False)
            with pe.Fori(2, NB) as i:
                row_3(i, True)
            t_row(NB - 1)

            def rows_back(r):
                pe.wait_ge(t_set, NB)
                pe.wait_ge(s0_read, NB + r)
                pe.wait_ge(rows_set, 2 * r + 2)
                for b in range(CH):
                    mm = pe.transpose(chunk(s0, b), chunk(xrow, b), ident[:])
                mm.then_inc(rows_ps, 1)
                pe.wait_ge(p12_set, 2 * r)
                for b in range(CH):
                    mm = pe.transpose(chunk(s1, b), chunk(trow, b), ident[:])
                mm.then_inc(rows_ps, 1)

            def out_row(r):
                pe.wait_ge(p12_set, 2 * r + 2)
                pe.wait_ge(t2_set, r + 1)
                for b in range(CH):
                    for n, src in enumerate((p1, p2, p0)):
                        mm = pe.matmul(chunk(s0, b), chunk(src, b), cheb[:, n * D:(n + 1) * D], start=(n == 0),
                                       stop=(n == 2), skip_group_check=True)
                mm.then_inc(out_ps, 1)

            for h in range(2):
                pe.wait_ge(turned[h], turned_4(0, 0) + 1)
                pe.wait_ge(a_taken[h], 2 * NB - 1)
                clear(acc_a, h)
                into_a(h, a_4(0, 0))
            rows_back(0)
            out_row(0)
            with pe.Fori(1, NB) as r:
                for h in range(2):
                    pe.wait_ge(turned[h], turned_4(r, 0) + 1)
                    pe.wait_ge(u_read, 2 * r - 1 + h)
                    clear(acc_a, h)
                    into_a(h, a_4(r, 0))
                with pe.Fori(1, r + 1) as m:
                    for h in range(2):
                        pe.wait_ge(turned[h], turned_4(r, m) + 1)
                        into_a(h, a_4(r, m))
                rows_back(r)
                out_row(r)


_INPUTS = ["x", "adj", "L0_gnn_W", "L0_gnn_b", "L1_gnn_weight", "L1_gnn_bias"]


def kernel(**inputs):
    import numpy as np
    import concourse.bacc as bacc
    from concourse.bass_utils import run_bass_kernel_spmd

    nc = bacc.Bacc("TRN2", target_bir_lowering=False, num_devices=1)
    arrays, args = {}, []
    for name in _INPUTS:
        a = np.ascontiguousarray(inputs[name])
        arrays[f"in_{name}"] = a
        args.append(nc.dram_tensor(f"in_{name}", a.shape, mybir.dt.from_np(a.dtype), kind="ExternalInput").ap())
    out = nc.dram_tensor("out_rows", arrays["in_x"].shape, F32, kind="ExternalOutput").ap()
    build(nc, *args, out)
    return run_bass_kernel_spmd(nc, [arrays], core_ids=[0]).results[0]["out_rows"]
```

```python
from contextlib import ExitStack

import concourse.bass as bass
from concourse import mybir

ALU = mybir.AluOpType
ACT = mybir.ActivationFunctionType
AX_X = mybir.AxisListType.X
F32 = mybir.dt.float32
F32R = mybir.dt.float32r
BF16 = mybir.dt.bfloat16

P = 128
Q = 32
NQ = P // Q
BLK = 1024
HALF = 512
CH = BLK // P
COLS_Q = BLK // NQ
GR = HALF // Q
TILE = HALF * BLK // P
STRIPS = HALF // P
DMAS = 4
COLS_T = COLS_Q // 2
GC = 2
NG = CH // GC
GSZ = GC * HALF
LN_EPS = 1e-5


def tri(n):
    return n * (n + 1) // 2


def build(nc, x, adj, w0, b0, w1, b1, out):
    N, D = x.shape
    NB = N // BLK
    assert D == P and adj.shape[0] == N and NB >= 2 * STRIPS and NB % 2 == 0

    WITH = tri(NB)
    STRICT = tri(NB - 1)
    def q_1(i, j): return tri(i - 2) + (i - 1) + j
    def q_2(r, m): return STRICT + tri(r) + m
    def q_3(i, j): return STRICT + WITH + tri(i) + j
    def q_4(r, m): return STRICT + 2 * WITH + tri(r) + m
    def a_1(i, j): return q_1(i, j)
    def a_2(r, m): return STRICT + tri(r) + m
    def a_3(i, j): return STRICT + WITH + tri(i - 1) + j
    def a_4(r, m): return 2 * STRICT + WITH + tri(r) + m
    def b_2(r, m): return tri(r - 1) + m
    def b_3(i, j): return STRICT + tri(i) + j

    MID = NB // 2

    with ExitStack() as ctx:
        def sb(name, shape, dt=F32):
            return ctx.enter_context(nc.sbuf_tensor(name, shape, dt))

        def ps(name, shape):
            return ctx.enter_context(nc.psum_tensor(name, shape, F32))

        def sem(name):
            return ctx.enter_context(nc.semaphore(name))

        nat = [sb(f"nat{t}", [P, TILE]) for t in range(2)]
        at = [sb(f"at{g}", [P, GSZ]) for g in range(NG)]
        high = [sb(f"high{g}", [P, GSZ], F32R) for g in range(NG)]
        low = [sb(f"low{k}", [P, GSZ], F32R) for k in range(2)]
        dx_t = sb("dx_t", [P, NB * BLK])
        x1 = sb("x1", [P, NB * BLK])
        part = sb("part", [P, NB * BLK])
        wa_h = sb("wa_h", [P, BLK], F32R)
        wa_l = sb("wa_l", [P, BLK], F32R)
        wb_h = sb("wb_h", [P, BLK], F32R)
        wb_l = sb("wb_l", [P, BLK], F32R)
        xrow = sb("xrow", [P, BLK])
        trow = sb("trow", [P, BLK])
        p0 = sb("p0", [P, BLK])
        z = sb("z", [P, BLK])
        w0t = sb("w0t", [P, D])
        cheb = sb("cheb", [P, 3 * D])
        bias0 = sb("bias0", [P, D])
        bias1 = sb("bias1", [P, D])
        ident = sb("ident", [P, P])
        ident_r = sb("ident_r", [P, P], F32R)
        ones_r = sb("ones_r", [P, P], F32R)
        same_q = [sb(f"same_q{q}", [P, P]) for q in range(NQ)]
        zeros = sb("zeros", [P, P], BF16)
        up_sum = sb("up_sum", [P, 2 * STRIPS * NB])
        zero_s = sb("zero_s", [P, 2 * STRIPS])
        up1 = sb("up1", [P, 2 * STRIPS])
        dcol = sb("dcol", [P, NB * CH])
        deg = sb("deg", [P, CH])
        is0 = sb("is0", [P, CH])
        safe = sb("safe", [P, CH])
        root = sb("root", [P, CH])
        mean = sb("mean", [P, CH])
        var = sb("var", [P, CH])
        rstd = sb("rstd", [P, CH])
        neg_half = sb("neg_half", [P, CH])

        acc_a = ps("acc_a", [P, 2, HALF])
        acc_b = ps("acc_b", [P, 2, HALF])
        s0 = ps("s0", [P, BLK])
        s1 = ps("s1", [P, BLK])

        const_in = sem("const_in")
        pool_const = sem("pool_const")
        dve_const = sem("dve_const")
        w0_turned = sem("w0_turned")
        tile_in = [sem(f"tile_in{h}") for h in range(2)]
        strips_in = [sem(f"strips_in{h}") for h in range(2)]
        strips_free = [sem(f"strips_free{h}") for h in range(2)]
        nat_free = [sem(f"nat_free{h}") for h in range(2)]
        turned = sem("turned")
        high_set = sem("high_set")
        low_dve = sem("low_dve")
        low_pool = sem("low_pool")
        used = sem("used")
        wa_high = sem("wa_high")
        wa_low = sem("wa_low")
        wb_high = sem("wb_high")
        wb_low = sem("wb_low")
        a_taken = [sem(f"a_taken{h}") for h in range(2)]
        b_taken = [sem(f"b_taken{h}") for h in range(2)]
        xrow_in = sem("xrow_in")
        xrow_read = sem("xrow_read")
        up_zeroed = sem("up_zeroed")
        sums_set = sem("sums_set")
        low_taken = sem("low_taken")
        deg_ps = sem("deg_ps")
        safe_set = sem("safe_set")
        root_set = sem("root_set")
        d_set = sem("d_set")
        dx_set = sem("dx_set")
        p0_set = sem("p0_set")
        part_zero = sem("part_zero")
        z_ps = sem("z_ps")
        s0_read = sem("s0_read")
        var_set = sem("var_set")
        rstd_set = sem("rstd_set")
        x1_set = sem("x1_set")
        t_ps = sem("t_ps")
        t_set = sem("t_set")
        rows_set = sem("rows_set")
        rows_ps = sem("rows_ps")
        p12_set = sem("p12_set")
        u_read = sem("u_read")
        t2_set = sem("t2_set")
        out_ps = sem("out_ps")
        y_set = sem("y_set")
        y_out = sem("y_out")
        steps1 = sem("steps1")
        steps2 = sem("steps2")
        steps4 = sem("steps4")
        own_wait = sem("own_wait")
        DVE_CONST = 4 + NQ + NQ + 2

        def alone(wait):
            wait.then_inc(own_wait, 1)

        def blockof(t, i):
            return t[:, bass.ds(i * BLK, BLK)]

        def halfof(t, i, h):
            return t[:, bass.ds(i * BLK + h * HALF, HALF)]

        def per_chunk(t):
            return t.rearrange("p (b d) -> p b d", b=CH)

        def over_features(t):
            return t.unsqueeze(2).broadcast_to([P, CH, D])

        def over_chunks(t):
            return t.unsqueeze(1).broadcast_to([P, CH, D])

        def packed(t, h):
            return t[:].rearrange("p (b a c) -> p a b c", b=CH, a=NQ)[:, 2 * h:2 * h + 2]

        def in_order(t):
            return t.rearrange("p (a b c) -> p a b c", a=2, b=CH)

        def node_rows(t, i, a):
            return t[bass.ds(i * BLK + a * COLS_Q, COLS_Q), :].rearrange("(b c) d -> c b d", c=Q)

        def wait(engine, semaphore, value):
            if not isinstance(value, int) or value > 0:
                engine.wait_ge(semaphore, value)

        def strip_of(h, s):
            return x1[:, (h * STRIPS + s) * BLK:(h * STRIPS + s + 1) * BLK]

        block = ctx.enter_context(nc.Block())

        @block.sync
        def _(sp):
            sp.dma_start(z[:, 0:D], w0).then_inc(const_in, 16)
            sp.dma_start(cheb[:].rearrange("p (k o) -> p k o", k=3), w1.rearrange("k d o -> d k o")).then_inc(const_in, 16)
            sp.dma_start(bias0[:], b0.partition_broadcast(P)).then_inc(const_in, 16)
            sp.dma_start(bias1[:], b1.partition_broadcast(P)).then_inc(const_in, 16)

            def free(semaphore, count):
                if not isinstance(count, int) or count > 0:
                    alone(sp.wait_ge(semaphore, count))

            def tile(t, i, j, q):
                free(nat_free[t], q)
                for a in range(NQ):
                    src = adj[bass.ds(i * BLK, BLK), bass.ds(j * BLK + a * COLS_Q + t * COLS_T, COLS_T)]
                    dst = nat[t][Q * a:Q * a + Q, :].rearrange("r (g c) -> r g c", g=2 * GR)
                    sp.dma_start(dst, src.rearrange("(g r) c -> r g c", r=Q)).then_inc(tile_in[t], 16)

            def square(i, j, q):
                for t in range(2):
                    tile(t, i, j, q)

            def strips(h, i, j, count):
                free(strips_free[h], count)
                for s in range(STRIPS):
                    src = adj[bass.ds(i * BLK + h * HALF + s * P, P), bass.ds(j * BLK, BLK)]
                    sp.dma_start(strip_of(h, s), src).then_inc(strips_in[h], 16)

            def row_1(i, more=None, strips_left=False):
                if more is None:
                    with sp.Fori(0, i) as m:
                        for t in range(2):
                            tile(t, i, m, q_1(i, m))
                            strips(t, i, NB - 1 - m, NB * i + m)
                    if strips_left:
                        with sp.Fori(0, NB - 2 * i) as e:
                            for h in range(2):
                                strips(h, i, i + e, NB * i + i + e)
                else:
                    with sp.Fori(0, more) as m:
                        square(i, m, q_1(i, m))
                    with sp.Fori(0, NB - i) as m:
                        for t in range(2):
                            tile(t, i, i - 1 - m, q_1(i, more + m))
                            strips(t, i, NB - 1 - m, NB * i + m)

            for h in range(2):
                strips(h, 0, 0, 0)
            with sp.Fori(1, NB) as j:
                for h in range(2):
                    strips(h, 0, j, j)
            row_1(1, strips_left=True)
            with sp.Fori(2, MID) as i:
                row_1(i, strips_left=True)
            row_1(MID)
            with sp.Fori(0, NB - MID - 1) as k:
                row_1(MID + 1 + k, 2 * k + 2)
            with sp.Fori(0, NB) as r:
                with sp.Fori(0, r + 1) as m:
                    square(NB - 1 - r, NB - 1 - m, q_2(r, m))
            with sp.Fori(0, NB) as i:
                with sp.Fori(0, i + 1) as j:
                    square(i, j, q_3(i, j))
            with sp.Fori(0, NB) as r:
                with sp.Fori(0, r + 1) as m:
                    square(NB - 1 - r, NB - 1 - m, q_4(r, m))

        @block.gpsimd
        def _(pool):
            nc.gpsimd.memset(ident[:], 0.0).then_inc(pool_const, 1)
            nc.gpsimd.memset(neg_half[:], -0.5).then_inc(pool_const, 1)
            pool.wait_ge(pool_const, 2)
            nc.gpsimd.affine_select(out=ident[:], in_=ident[:], compare_op=ALU.not_equal, fill=1.0, base=0,
                                    pattern=[[-1, P]], channel_multiplier=1).then_inc(pool_const, 1)

            def load_x(i):
                for a in range(NQ):
                    dst = xrow[Q * a:Q * a + Q, :].rearrange("c (b d) -> c b d", b=CH)
                    pool.dma_start(dst, node_rows(x, i, a)).then_inc(xrow_in, 16)

            def power(dst, src, signal):
                nc.gpsimd.tensor_tensor(dst[:], src[:], neg_half[:], ALU.pow).then_inc(signal, 1)

            def low_group(q, h, g, first=False):
                pool.wait_ge(high_set, 2 * NG * q + NG * h + g + 1)
                if not (first and h == 0 and g < 2):
                    pool.wait_ge(used, 2 * NG * q + NG * h + g - 1)
                nc.gpsimd.tensor_tensor(low[g % 2][:], at[g][:], high[g][:].bitcast(F32), ALU.subtract).then_inc(low_pool, 1)

            def low_half(w_h, w_l, src, row, half, w_high, w_low, blocks):
                alone(pool.wait_ge(w_high, 2 * blocks + half + 1))
                part_ = slice(half * HALF, (half + 1) * HALF)
                nc.gpsimd.tensor_tensor(w_l[:, part_], halfof(src, row, half), w_h[:, part_].bitcast(F32),
                                        ALU.subtract).then_inc(w_low, 1)

            def low_block(q, row, a=None, b=None, first=False):
                for t in range(2):
                    if a is not None:
                        low_half(wa_h, wa_l, dx_t, row, t, wa_high, wa_low, a)
                    if b is not None:
                        low_half(wb_h, wb_l, x1, row, t, wb_high, wb_low, b)
                    low_group(q, t, 1, first)
                    low_group(q, t, 3)

            load_x(0)
            pool.wait_ge(safe_set, 1)
            power(root, safe, root_set)
            pool.wait_ge(dx_set, 1)
            load_x(1)
            low_block(0, 0, a=0, first=True)
            pool.wait_ge(safe_set, 2)
            power(root, safe, root_set)

            def row_1(i, more):
                alone(pool.wait_ge(dx_set, i))
                load_x(i)
                with pool.Fori(0, more if more is not None else i) as j:
                    low_block(q_1(i, j), j, a=a_1(i, j))
                if more is not None:
                    with pool.Fori(0, NB - i) as m:
                        low_block(q_1(i, more + m), i - 1 - m, a=a_1(i, more + m))
                pool.wait_ge(safe_set, i + 1)
                power(root, safe, root_set)

            with pool.Fori(2, MID + 1) as i:
                row_1(i, None)
            with pool.Fori(0, NB - MID - 1) as k:
                row_1(MID + 1 + k, 2 * k + 2)
            pool.wait_ge(dx_set, NB)
            load_x(NB - 1)
            low_block(q_2(0, 0), NB - 1, a=a_2(0, 0))
            pool.wait_ge(var_set, 1)
            power(rstd, var, rstd_set)
            pool.wait_ge(xrow_read, 1)
            load_x(NB - 2)
            low_block(q_2(1, 0), NB - 1, a=a_2(1, 0), b=b_2(1, 0))
            low_block(q_2(1, 1), NB - 2, a=a_2(1, 1))
            with pool.Fori(2, NB) as r:
                low_block(q_2(r, 0), NB - 1, a=a_2(r, 0), b=b_2(r, 0))
                pool.wait_ge(var_set, r)
                power(rstd, var, rstd_set)
                alone(pool.wait_ge(xrow_read, r))
                load_x(NB - 1 - r)
                with pool.Fori(1, r) as m:
                    low_block(q_2(r, m), NB - 1 - m, a=a_2(r, m), b=b_2(r, m))
                low_block(q_2(r, r), NB - 1 - r, a=a_2(r, r))
            pool.wait_ge(var_set, NB)
            power(rstd, var, rstd_set)
            low_block(q_3(0, 0), 0, b=b_3(0, 0))
            low_block(q_3(1, 0), 0, a=a_3(1, 0), b=b_3(1, 0))
            low_block(q_3(1, 1), 1, b=b_3(1, 1))
            with pool.Fori(2, NB) as i:
                with pool.Fori(0, i) as j:
                    low_block(q_3(i, j), j, a=a_3(i, j), b=b_3(i, j))
                low_block(q_3(i, i), i, b=b_3(i, i))

            def finish(r):
                pool.wait_ge(var_set, NB + r + 1)
                power(rstd, var, rstd_set)
                alone(pool.wait_ge(y_set, r + 1))
                for a in range(NQ):
                    src = z[Q * a:Q * a + Q, :].rearrange("c (b d) -> c b d", b=CH)
                    pool.dma_start(node_rows(out, NB - 1 - r, a), src).then_inc(y_out, 16)

            low_block(q_4(0, 0), NB - 1, a=a_4(0, 0))
            with pool.Fori(1, NB) as r:
                low_block(q_4(r, 0), NB - 1, a=a_4(r, 0))
                finish(r - 1)
                with pool.Fori(1, r + 1) as m:
                    low_block(q_4(r, m), NB - 1 - m, a=a_4(r, m))
            finish(NB - 1)
            pool.wait_ge(y_out, 16 * NQ * NB)

        @block.scalar
        def _(act):
            def copy(dst, src):
                return nc.scalar.activation(dst, src, ACT.Copy)

            def high_group(q, h, g, first=False):
                act.wait_ge(turned, 2 * NG * q + NG * h + g + 1)
                if h == 1 or not first:
                    act.wait_ge(used, 2 * NG * q + NG * (h - 1) + g + 1)
                copy(high[g][:], at[g][:]).then_inc(high_set, 1)

            def high_half(w_h, src, row, t, w_high, last):
                if last is not None:
                    act.wait_ge(used, 2 * NG * last + NG * (t + 1))
                part_ = slice(t * HALF, (t + 1) * HALF)
                copy(w_h[:, part_], halfof(src, row, t)).then_inc(w_high, 1)

            def high_block(q, row, a=None, b=None, first=False, between=None, beside=None):
                for t in range(2):
                    if a is not None:
                        high_half(wa_h, dx_t, row, t, wa_high, a if a is not False else None)
                    if b is not None:
                        high_half(wb_h, x1, row, t, wb_high, b if b is not False else None)
                    for g in range(NG):
                        high_group(q, t, g, first)
                        if beside is not None:
                            beside(t, g)
                        if (t, g) == (0, 1) and between is not None:
                            between(0)
                            between(1)
                    act.sem_inc(nat_free[t], 1)

            ups = up_sum[:].rearrange("p (s j) -> p s j", j=NB)

            def strip(h, s, j, count):
                if s == 0:
                    act.wait_ge(strips_in[h], 16 * DMAS * (count + 1))
                summed = nc.scalar.activation(strip_of(h, s), strip_of(h, s), ACT.Copy,
                                              accum_out=ups[:, STRIPS * h + s, bass.ds(j, 1)])
                if s == STRIPS - 1:
                    summed.then_inc(strips_free[h], 1)

            def strips(j, count):
                for h in range(2):
                    for s in range(STRIPS):
                        strip(h, s, j, count)

            def take_h(i, h):
                act.wait_ge(used, 2 * NG * q_1(i, i) - 1 + h)
                copy(halfof(part, i, h), acc_a[:, h]).then_inc(a_taken[h], 1)

            def row_1(i, more=None, strips_left=False):
                act.wait_ge(sums_set, i)
                copy(ups[:, :, bass.ds(i - 1, 1)], zero_s[:].unsqueeze(2)).then_inc(up_zeroed, 1)
                first = isinstance(i, int) and i == 1

                def block_1(place, j, beside=None):
                    q = q_1(i, place)
                    high_block(q, j, a=False if first else q - 1, first=first, beside=beside)

                def pair(m, place, j):
                    block_1(place, j, beside=lambda t, g: strip(t, g, NB - 1 - m, NB * i + m))

                if first:
                    act.wait_ge(dx_set, 1)
                    pair(0, 0, 0)
                elif more is None:
                    with act.Fori(0, i) as m:
                        act.wait_ge(dx_set, m + 1)
                        pair(m, m, m)
                else:
                    with act.Fori(0, more) as m:
                        block_1(m, m)
                    act.wait_ge(dx_set, i)
                    with act.Fori(0, NB - i) as m:
                        pair(m, more + m, i - 1 - m)
                if strips_left:
                    with act.Fori(0, NB - 2 * i) as e:
                        strips(i + e, NB * i + i + e)
                with act.Fori(0, i):
                    for h in range(2):
                        act.sem_inc(strips_in[h], 16 * DMAS)
                        act.sem_inc(strips_free[h], 1)
                take_h(i, 0)
                take_h(i, 1)

            act.wait_ge(dve_const, DVE_CONST)
            with act.Fori(0, NB) as j:
                strips(j, j)
            row_1(1, strips_left=True)
            with act.Fori(2, MID) as i:
                row_1(i, strips_left=True)
            row_1(MID)
            with act.Fori(0, NB - MID - 1) as k:
                row_1(MID + 1 + k, 2 * k + 2)

            def take_b(r, h):
                act.wait_ge(p0_set, 2 * r + h + 1)
                copy(halfof(part, NB - 1 - r, h), acc_b[:, h]).then_inc(b_taken[h], 1)

            act.wait_ge(dx_set, NB)
            high_block(q_2(0, 0), NB - 1, a=q_2(0, 0) - 1)
            act.wait_ge(x1_set, 1)
            high_block(q_2(1, 0), NB - 1, a=q_2(1, 0) - 1, b=False)
            high_block(q_2(1, 1), NB - 2, a=q_2(1, 1) - 1)
            with act.Fori(2, NB) as r:
                high_block(q_2(r, 0), NB - 1, a=q_2(r, 0) - 1, b=q_2(r, 0) - 2, between=lambda h: take_b(r - 1, h))
                with act.Fori(1, r) as m:
                    act.wait_ge(x1_set, m + 1)
                    high_block(q_2(r, m), NB - 1 - m, a=q_2(r, m) - 1, b=q_2(r, m) - 1)
                high_block(q_2(r, r), NB - 1 - r, a=q_2(r, r) - 1)
            take_b(NB - 1, 0)
            take_b(NB - 1, 1)

            def take_t(i):
                act.wait_ge(t_ps, i + 1)
                copy(blockof(dx_t, i), s0[:]).then_inc(t_set, 1)
                act.wait_ge(t_set, i + 1)

            def take_u(i, h):
                act.wait_ge(p0_set, 2 * NB + 2 * i + h + 1)
                copy(halfof(part, i, h), acc_a[:, h]).then_inc(a_taken[h], 1)

            act.wait_ge(x1_set, NB)
            high_block(q_3(0, 0), 0, b=q_3(0, 0) - 2)
            take_t(0)
            high_block(q_3(1, 0), 0, a=q_3(1, 0) - 2, b=q_3(1, 0) - 1)
            high_block(q_3(1, 1), 1, b=q_3(1, 1) - 1)
            with act.Fori(2, NB) as i:
                high_block(q_3(i, 0), 0, a=q_3(i, 0) - 2, b=q_3(i, 0) - 1, between=lambda h: take_u(i - 1, h))
                take_t(i - 1)
                with act.Fori(1, i) as j:
                    high_block(q_3(i, j), j, a=q_3(i, j) - 1, b=q_3(i, j) - 1)
                high_block(q_3(i, i), i, b=q_3(i, i) - 1)
            take_u(NB - 1, 0)
            take_u(NB - 1, 1)
            take_t(NB - 1)

            def stage_rows(r):
                if not isinstance(r, int):
                    act.wait_ge(out_ps, r)
                copy(xrow[:], blockof(x1, NB - 1 - r)).then_inc(rows_set, 1)
                copy(trow[:], blockof(dx_t, NB - 1 - r)).then_inc(rows_set, 1)

            def take_rows(r):
                act.wait_ge(rows_ps, 2 * r + 1)
                copy(xrow[:], s0[:]).then_inc(p12_set, 1)
                act.wait_ge(rows_ps, 2 * r + 2)
                copy(trow[:], s1[:]).then_inc(p12_set, 1)

            act.wait_ge(xrow_read, NB)
            high_block(q_4(0, 0), NB - 1, a=q_4(0, 0) - 2)
            stage_rows(0)
            take_rows(0)
            with act.Fori(1, NB) as r:
                high_block(q_4(r, 0), NB - 1, a=q_4(r, 0) - 1)
                stage_rows(r)
                with act.Fori(1, r + 1) as m:
                    high_block(q_4(r, m), NB - 1 - m, a=q_4(r, m) - 1)
                take_rows(r)

        @block.vector
        def _(dve):
            nc.vector.memset(zero_s[:], 0.0).then_inc(dve_const, 1)
            nc.vector.memset(zeros[:], 0.0).then_inc(dve_const, 1)
            nc.vector.memset(ones_r[:].bitcast(F32), 1.0).then_inc(dve_const, 1)
            nc.vector.memset(blockof(part, 0), 0.0).then_inc(dve_const, 1)
            for q in range(NQ):
                nc.vector.memset(same_q[q][:], 0.0).then_inc(dve_const, 1)
            dve.wait_ge(pool_const, 3)
            dve.wait_ge(dve_const, 4 + NQ)
            for q in range(NQ):
                rows = slice(Q * q, Q * q + Q)
                corner = ident[rows, Q * q:Q * q + Q].unsqueeze(1).broadcast_to([Q, NQ, Q])
                nc.vector.tensor_copy(same_q[q][rows, :].rearrange("p (a c) -> p a c", a=NQ), corner).then_inc(dve_const, 1)
            nc.vector.tensor_copy(ident_r[:], ident[:]).then_inc(dve_const, 1)
            dve.wait_ge(w0_turned, 1)
            nc.vector.tensor_copy(w0t[:], s1[:, 0:D]).then_inc(dve_const, 1)

            def own_order(signal, start):
                count = [0]

                def step(ins):
                    count[0] += 1
                    ins.then_inc(signal, 1)
                    dve.wait_ge(signal, start + count[0])
                return step

            def turn(q, h, g, first=False):
                if h == 1 or not first:
                    if g % 2:
                        dve.wait_ge(low_pool, NG * q + NG // 2 * (h - 1) + g // 2 + 1)
                    else:
                        dve.wait_ge(low_dve, NG * q + NG // 2 * (h - 1) + g // 2 + 1)
                half, pair = g % 2, g // 2
                src = nat[h][:].rearrange("p (g b c) -> p g b c", g=2 * GR, b=CH // 2)
                src = src[:, GR * half:GR * (half + 1), GC * pair:GC * (pair + 1)]
                dst = at[g][:].rearrange("p (b g r) -> p g b r", b=GC, g=GR)
                nc.vector.transpose(dst, src).then_inc(turned, 1)

            def low_group(q, h, g, first=False):
                dve.wait_ge(high_set, 2 * NG * q + NG * h + g + 1)
                if not (first and h == 0 and g < 2):
                    dve.wait_ge(used, 2 * NG * q + NG * h + g - 1)
                nc.vector.tensor_tensor(low[g % 2][:], at[g][:], high[g][:].bitcast(F32), ALU.subtract).then_inc(low_dve, 1)

            def tile(q, h, first=False, between=None):
                dve.wait_ge(tile_in[h], 16 * DMAS * (q + 1))
                for g in range(0, NG, 2):
                    turn(q, h, g, first)
                    turn(q, h, g + 1, first)
                    if g == 0 and between is not None:
                        between(0)
                    low_group(q, h, g, first)
                    if g == 0 and between is not None:
                        between(1)

            def both(q, first=False, between=None):
                tile(q, 0, first, between)
                tile(q, 1, first)

            STEPS1 = NQ + 3

            def row_1(i):
                step = own_order(steps1, STEPS1 * i)
                lower = not isinstance(i, int) or i > 0
                if lower:
                    for h in range(2):
                        dve.wait_ge(used, 2 * NG * q_1(i, i) - 1 + h)
                        if not isinstance(i, int):
                            dve.wait_ge(deg_ps, i)
                        nc.vector.tensor_copy(packed(p0, h), in_order(acc_b[:, h])).then_inc(low_taken, 1)
                for h in range(2):
                    dve.wait_ge(strips_free[h], NB * i + NB)
                if lower:
                    dve.wait_ge(up_zeroed, i)
                nc.vector.tensor_reduce(up1[:], ups, AX_X, ALU.add).then_inc(sums_set, 1)
                dve.wait_ge(deg_ps, i + 1)
                for a in range(NQ):
                    rows = slice(Q * a, Q * a + Q)
                    step(nc.vector.tensor_scalar(deg[rows, :], s1[rows, CH * a:CH * a + CH], 1.0, None, ALU.add))
                if lower:
                    step(nc.vector.tensor_tensor(deg[:], deg[:], s1[:, 2 * GR:2 * GR + CH], ALU.add))
                else:
                    step(nc.vector.tensor_scalar(deg[:], deg[:], 0.0, None, ALU.add))
                step(nc.vector.tensor_scalar(is0[:], deg[:], 0.0, None, ALU.is_equal))
                nc.vector.tensor_tensor(safe[:], deg[:], is0[:], ALU.add).then_inc(safe_set, 1)
                dve.wait_ge(safe_set, i + 1)
                step(nc.vector.tensor_scalar(is0[:], is0[:], -1.0, 1.0, ALU.mult, ALU.add))
                dve.wait_ge(root_set, i + 1)
                d_i = dcol[:, bass.ds(i * CH, CH)]
                nc.vector.tensor_tensor(d_i, root[:], is0[:], ALU.mult).then_inc(d_set, 1)
                dve.wait_ge(d_set, i + 1)
                dve.wait_ge(xrow_in, 16 * NQ * (i + 1))
                nc.vector.tensor_tensor(per_chunk(blockof(dx_t, i)), per_chunk(xrow[:]), over_features(d_i),
                                        ALU.mult).then_inc(dx_set, 1)

            ups = up_sum[:].rearrange("p (s j) -> p s j", j=NB)
            row_1(0)
            both(0, first=True)
            row_1(1)
            with dve.Fori(2, NB) as i:
                with dve.Fori(0, i) as j:
                    both(q_1(i, j))
                row_1(i)

            def norm(step, rows, dst, signal, first=0):
                step(nc.vector.tensor_reduce(mean[:], per_chunk(z[:]), AX_X, ALU.add))
                step(nc.vector.tensor_scalar(mean[:], mean[:], 1.0 / D, None, ALU.mult))
                step(nc.vector.tensor_tensor(per_chunk(z[:]), per_chunk(z[:]), over_features(mean[:]), ALU.subtract))
                step(nc.vector.tensor_tensor(p0[:], z[:], z[:], ALU.mult))
                step(nc.vector.tensor_reduce(var[:], per_chunk(p0[:]), AX_X, ALU.add))
                nc.vector.tensor_scalar(var[:], var[:], 1.0 / D, LN_EPS, ALU.mult, ALU.add).then_inc(var_set, 1)
                dve.wait_ge(rstd_set, rows + 1)
                nc.vector.tensor_tensor(per_chunk(dst), per_chunk(z[:]), over_features(rstd[:]),
                                        ALU.mult).then_inc(signal, 1)
                alone(dve.wait_ge(signal, rows + 1 - first))

            STEPS2 = 6

            def h_half(r, h):
                alone(dve.wait_ge(used, 2 * NG * q_2(r, r) + 2 * NG - 1 + h))
                nc.vector.tensor_tensor(packed(p0, h), in_order(acc_a[:, h]), in_order(halfof(part, NB - 1 - r, h)),
                                        ALU.add).then_inc(p0_set, 1)

            def norm_0(r):
                step = own_order(steps2, STEPS2 * r)
                i = NB - 1 - r
                dve.wait_ge(z_ps, r + 1)
                nc.vector.tensor_tensor(per_chunk(z[:]), per_chunk(s0[:]), over_features(dcol[:, bass.ds(i * CH, CH)]),
                                        ALU.mult).then_inc(s0_read, 1)
                dve.wait_ge(s0_read, r + 1)
                dve.wait_ge(xrow_in, 16 * NQ * (NB + r + 1))
                nc.vector.tensor_tensor(z[:], z[:], xrow[:], ALU.add).then_inc(xrow_read, 1)
                dve.wait_ge(xrow_read, r + 1)
                step(nc.vector.tensor_tensor(per_chunk(z[:]), per_chunk(z[:]), over_chunks(bias0[:]), ALU.add))
                norm(step, r, blockof(x1, i), x1_set)

            for h in range(2):
                dve.wait_ge(a_taken[h], NB - 1)
            both(q_2(0, 0))
            h_half(0, 0)
            h_half(0, 1)
            dve.wait_ge(p0_set, 2)
            nc.vector.memset(blockof(part, NB - 1), 0.0).then_inc(part_zero, 1)
            norm_0(0)
            both(q_2(1, 0))
            both(q_2(1, 1))
            with dve.Fori(2, NB) as r:
                both(q_2(r, 0), between=lambda h: h_half(r - 1, h))
                norm_0(r - 1)
                with dve.Fori(1, r + 1) as m:
                    both(q_2(r, m))
            h_half(NB - 1, 0)
            h_half(NB - 1, 1)
            norm_0(NB - 1)

            def t_half(i, h):
                if not isinstance(i, int) or i > 0:
                    dve.wait_ge(t_ps, i)
                alone(dve.wait_ge(used, 2 * NG * q_3(i, i) + 2 * NG - 1 + h))
                nc.vector.tensor_tensor(packed(p0, h), in_order(acc_b[:, h]), in_order(halfof(part, i, h)),
                                        ALU.add).then_inc(p0_set, 1)

            dve.wait_ge(part_zero, 1)
            for h in range(2):
                dve.wait_ge(b_taken[h], NB - 1)
            both(q_3(0, 0))
            t_half(0, 0)
            t_half(0, 1)
            dve.wait_ge(p0_set, 2 * NB + 2)
            nc.vector.memset(blockof(part, 0), 0.0).then_inc(part_zero, 1)
            both(q_3(1, 0))
            both(q_3(1, 1))
            with dve.Fori(2, NB) as i:
                both(q_3(i, 0), between=lambda h: t_half(i - 1, h))
                with dve.Fori(1, i + 1) as j:
                    both(q_3(i, j))
            t_half(NB - 1, 0)
            t_half(NB - 1, 1)

            STEPS4 = 6

            def u_half(r, h):
                alone(dve.wait_ge(used, 2 * NG * q_4(r, r) + 2 * NG - 1 + h))
                nc.vector.tensor_tensor(packed(p0, h), in_order(acc_a[:, h]), in_order(halfof(part, NB - 1 - r, h)),
                                        ALU.add).then_inc(u_read, 1)

            def t2(r):
                dve.wait_ge(u_read, 2 * r + 2)
                dve.wait_ge(p12_set, 2 * r + 1)
                nc.vector.scalar_tensor_tensor(out=p0[:], in0=p0[:], scalar=2.0, in1=xrow[:], op0=ALU.mult,
                                               op1=ALU.subtract).then_inc(t2_set, 1)

            def norm_1(r):
                step = own_order(steps4, STEPS4 * r)
                dve.wait_ge(out_ps, r + 1)
                if not isinstance(r, int) or r > 0:
                    dve.wait_ge(y_out, 16 * NQ * r)
                nc.vector.tensor_tensor(z[:], s0[:], blockof(x1, NB - 1 - r), ALU.add).then_inc(s0_read, 1)
                dve.wait_ge(s0_read, NB + r + 1)
                step(nc.vector.tensor_tensor(per_chunk(z[:]), per_chunk(z[:]), over_chunks(bias1[:]), ALU.add))
                norm(step, NB + r, z[:], y_set, NB)

            dve.wait_ge(t_ps, NB)
            dve.wait_ge(part_zero, 2)
            for h in range(2):
                dve.wait_ge(a_taken[h], 2 * NB - 2)
            both(q_4(0, 0))

            def row_4(r):
                tile(q_4(r, 0), 0, between=lambda h: u_half(r - 1, h))
                t2(r - 1)
                tile(q_4(r, 0), 1)
                norm_1(r - 1)
                with dve.Fori(1, r + 1) as m:
                    both(q_4(r, m))

            row_4(1)
            with dve.Fori(2, NB) as r:
                row_4(r)
            u_half(NB - 1, 0)
            u_half(NB - 1, 1)
            t2(NB - 1)
            norm_1(NB - 1)

        @block.tensor
        def _(pe):
            def chunk(t, b):
                return t[:, b * P:(b + 1) * P]

            def clear(acc, h):
                for b in range(HALF // P):
                    pe.matmul(acc[:, h, b * P:(b + 1) * P], zeros[:], zeros[:], start=(b == 0), stop=False,
                              skip_group_check=True)

            def add(to, w, m, stop=False):
                return pe.matmul(to, w, m, start=False, stop=stop, skip_group_check=True)

            def tile(q, t, a=None, b=None, sums=False, diagonal=False, opening=None):
                for g in range(NG):
                    h, pair = g % 2, g // 2
                    if g < 2 and opening is not None:
                        opening(h)
                    pe.wait_ge(high_set, 2 * NG * q + NG * t + g + 1)
                    products = [(acc_b, wb_h, wb_l, wb_low, b), (acc_a, wa_h, wa_l, wa_low, a)]
                    products = [p for p in products if p[-1] is not None]
                    for acc, w_h, w_l, w_low, blocks in products:
                        if g == 0:
                            pe.wait_ge(w_low, 2 * blocks + t + 1)
                        for c in range(GC):
                            ch = CH // 2 * t + GC * pair + c
                            cols = slice(c * HALF, (c + 1) * HALF)
                            if diagonal:
                                to = acc[:, h].rearrange("p (a b c) -> p a b c", a=2, b=CH)[:, :, ch]
                                eye = ident_r[:, 2 * Q * h:2 * Q * (h + 1)].rearrange("p (a c) -> p a c", a=2)
                                add(to, chunk(w_h, ch), eye)
                                add(to, chunk(w_l, ch), eye)
                            add(acc[:, h], chunk(w_h, ch), high[g][:, cols])
                            add(acc[:, h], chunk(w_l, ch), high[g][:, cols])
                    if sums:
                        for c in range(GC):
                            add(acc_b[:, h], ones_r[:], high[g][:, c * HALF:(c + 1) * HALF])
                    pe.wait_ge(low_pool if g % 2 else low_dve, NG * q + NG // 2 * t + g // 2 + 1)
                    for c in range(GC):
                        cols = slice(c * HALF, (c + 1) * HALF)
                        for acc, w_h, w_l, w_low, blocks in products:
                            last = add(acc[:, h], chunk(w_h, CH // 2 * t + GC * pair + c), low[g % 2][:, cols], stop=True)
                        if sums:
                            last = add(acc_b[:, h], ones_r[:], low[g % 2][:, cols], stop=True)
                    last.then_inc(used, 1)

            pe.wait_ge(const_in, 16 * 4)
            pe.wait_ge(pool_const, 3)
            pe.transpose(s1[:, 0:D], z[:, 0:D], ident[:]).then_inc(w0_turned, 1)
            pe.wait_ge(dve_const, DVE_CONST)

            def degrees(i):
                pe.wait_ge(sums_set, i + 1)
                for q in range(NQ):
                    to = s1[:, 0:2 * GR].rearrange("p (s q) -> p q s", q=NQ)[:, q]
                    mm = pe.matmul(to, same_q[q][:], up1[:], start=(q == 0), stop=(q == NQ - 1), skip_group_check=True)
                if not isinstance(i, int) or i > 0:
                    pe.wait_ge(low_taken, 2 * i)
                    for b in range(CH):
                        mm = add(s1[:, 2 * GR + b:2 * GR + b + 1], chunk(p0, b), ident[:, 0:1], stop=True)
                mm.then_inc(deg_ps, 1)

            degrees(0)
            for h in range(2):
                clear(acc_a, h)
                clear(acc_b, h)
            for t in range(2):
                tile(0, t, a=0, sums=True)
            degrees(1)
            with pe.Fori(2, NB) as i:
                def opening(h):
                    pe.wait_ge(a_taken[h], i - 1)
                    clear(acc_a, h)
                    pe.wait_ge(low_taken, 2 * i - 2)
                    clear(acc_b, h)

                tile(q_1(i, 0), 0, a=a_1(i, 0), sums=True, opening=opening)
                tile(q_1(i, 0), 1, a=a_1(i, 0), sums=True)
                with pe.Fori(1, i) as j:
                    for t in range(2):
                        tile(q_1(i, j), t, a=a_1(i, j), sums=True)
                degrees(i)

            def z_row(r):
                pe.wait_ge(p0_set, 2 * r + 2)
                if not isinstance(r, int) or r > 0:
                    pe.wait_ge(s0_read, r)
                for b in range(CH):
                    mm = pe.matmul(chunk(s0, b), chunk(p0, b), w0t[:], start=True, stop=True, skip_group_check=True)
                mm.then_inc(z_ps, 1)

            for h in range(2):
                pe.wait_ge(a_taken[h], NB - 1)
                clear(acc_a, h)
            for t in range(2):
                tile(q_2(0, 0), t, a=a_2(0, 0), diagonal=True)
            z_row(0)
            for h in range(2):
                clear(acc_a, h)
                pe.wait_ge(low_taken, 2 * NB - 2)
                clear(acc_b, h)
            for t in range(2):
                tile(q_2(1, 0), t, a=a_2(1, 0), b=b_2(1, 0))
            for t in range(2):
                tile(q_2(1, 1), t, a=a_2(1, 1), diagonal=True)
            with pe.Fori(2, NB) as r:
                def opening(h):
                    pe.wait_ge(p0_set, 2 * r - 1 + h)
                    clear(acc_a, h)
                    pe.wait_ge(b_taken[h], r - 1)
                    clear(acc_b, h)

                tile(q_2(r, 0), 0, a=a_2(r, 0), b=b_2(r, 0), opening=opening)
                z_row(r - 1)
                tile(q_2(r, 0), 1, a=a_2(r, 0), b=b_2(r, 0))
                with pe.Fori(1, r) as m:
                    for t in range(2):
                        tile(q_2(r, m), t, a=a_2(r, m), b=b_2(r, m))
                for t in range(2):
                    tile(q_2(r, r), t, a=a_2(r, r), diagonal=True)
            z_row(NB - 1)

            def t_row(i):
                pe.wait_ge(p0_set, 2 * NB + 2 * i + 2)
                if isinstance(i, int) and i == 0:
                    pe.wait_ge(s0_read, NB)
                else:
                    pe.wait_ge(t_set, i)
                for b in range(CH):
                    mm = pe.transpose(chunk(s0, b), chunk(p0, b), ident[:])
                mm.then_inc(t_ps, 1)

            for h in range(2):
                pe.wait_ge(b_taken[h], NB - 1)
                clear(acc_b, h)
            for t in range(2):
                tile(q_3(0, 0), t, b=b_3(0, 0))
            t_row(0)
            for h in range(2):
                clear(acc_b, h)
                clear(acc_a, h)
            for t in range(2):
                tile(q_3(1, 0), t, a=a_3(1, 0), b=b_3(1, 0))
            for t in range(2):
                tile(q_3(1, 1), t, b=b_3(1, 1))
            with pe.Fori(2, NB) as i:
                def opening(h):
                    pe.wait_ge(p0_set, 2 * NB + 2 * i - 1 + h)
                    clear(acc_b, h)
                    pe.wait_ge(a_taken[h], NB - 1 + i - 1)
                    clear(acc_a, h)

                tile(q_3(i, 0), 0, a=a_3(i, 0), b=b_3(i, 0), opening=opening)
                t_row(i - 1)
                tile(q_3(i, 0), 1, a=a_3(i, 0), b=b_3(i, 0))
                with pe.Fori(1, i) as j:
                    for t in range(2):
                        tile(q_3(i, j), t, a=a_3(i, j), b=b_3(i, j))
                for t in range(2):
                    tile(q_3(i, i), t, b=b_3(i, i))
            t_row(NB - 1)

            def rows_back(r):
                pe.wait_ge(s0_read, NB + r)
                pe.wait_ge(rows_set, 2 * r + 2)
                for b in range(CH):
                    mm = pe.transpose(chunk(s0, b), chunk(xrow, b), ident[:])
                mm.then_inc(rows_ps, 1)
                for b in range(CH):
                    mm = pe.transpose(chunk(s1, b), chunk(trow, b), ident[:])
                mm.then_inc(rows_ps, 1)

            def out_row(r):
                pe.wait_ge(p12_set, 2 * r + 2)
                pe.wait_ge(t2_set, r + 1)
                for b in range(CH):
                    for n, src in enumerate((xrow, trow, p0)):
                        mm = pe.matmul(chunk(s0, b), chunk(src, b), cheb[:, n * D:(n + 1) * D], start=(n == 0),
                                       stop=(n == 2), skip_group_check=True)
                mm.then_inc(out_ps, 1)

            for h in range(2):
                pe.wait_ge(a_taken[h], 2 * NB - 2)
                clear(acc_a, h)
            for t in range(2):
                tile(q_4(0, 0), t, a=a_4(0, 0))
            pe.wait_ge(t_set, NB)
            rows_back(0)
            with pe.Fori(1, NB) as r:
                def opening(h):
                    pe.wait_ge(u_read, 2 * r - 1 + h)
                    clear(acc_a, h)

                tile(q_4(r, 0), 0, a=a_4(r, 0), opening=opening)
                out_row(r - 1)
                tile(q_4(r, 0), 1, a=a_4(r, 0))
                rows_back(r)
                with pe.Fori(1, r + 1) as m:
                    for t in range(2):
                        tile(q_4(r, m), t, a=a_4(r, m))
            out_row(NB - 1)


_INPUTS = ["x", "adj", "L0_gnn_W", "L0_gnn_b", "L1_gnn_weight", "L1_gnn_bias"]


def kernel(**inputs):
    import numpy as np
    import concourse.bacc as bacc
    from concourse.bass_utils import run_bass_kernel_spmd

    nc = bacc.Bacc("TRN2", target_bir_lowering=False, num_devices=1)
    arrays, args = {}, []
    for name in _INPUTS:
        a = np.ascontiguousarray(inputs[name])
        arrays[f"in_{name}"] = a
        args.append(nc.dram_tensor(f"in_{name}", a.shape, mybir.dt.from_np(a.dtype), kind="ExternalInput").ap())
    out = nc.dram_tensor("out_rows", arrays["in_x"].shape, F32, kind="ExternalOutput").ap()
    build(nc, *args, out)
    return run_bass_kernel_spmd(nc, [arrays], core_ids=[0]).results[0]["out_rows"]
```

```python
from contextlib import ExitStack

import concourse.bass as bass
from concourse import mybir

ALU = mybir.AluOpType
ACT = mybir.ActivationFunctionType
AX_X = mybir.AxisListType.X
F32 = mybir.dt.float32
F32R = mybir.dt.float32r
BF16 = mybir.dt.bfloat16

P = 128
Q = 32
NQ = P // Q
BLK = 1024
HALF = 512
CH = BLK // P
COLS_Q = BLK // NQ
GR = HALF // Q
TILE = HALF * BLK // P
STRIPS = HALF // P
DMAS = 4
COLS_T = COLS_Q // 2
GC = 2
NG = CH // GC
GSZ = GC * HALF
LN_EPS = 1e-5


def tri(n):
    return n * (n + 1) // 2


def build(nc, x, adj, w0, b0, w1, b1, out):
    N, D = x.shape
    NB = N // BLK
    assert D == P and adj.shape[0] == N and NB >= 2 * STRIPS and NB % 2 == 0

    WITH = tri(NB)
    STRICT = tri(NB - 1)
    def q_1(i, j): return tri(i - 2) + (i - 1) + j
    def q_2(r, m): return STRICT + tri(r) + m
    def q_3(i, j): return STRICT + WITH + tri(i) + j
    def q_4(r, m): return STRICT + 2 * WITH + tri(r) + m
    def a_1(i, j): return q_1(i, j)
    def a_2(r, m): return STRICT + tri(r) + m
    def a_3(i, j): return STRICT + WITH + tri(i - 1) + j
    def a_4(r, m): return 2 * STRICT + WITH + tri(r) + m
    def b_2(r, m): return tri(r - 1) + m
    def b_3(i, j): return STRICT + tri(i) + j

    MID = NB // 2

    with ExitStack() as ctx:
        def sb(name, shape, dt=F32):
            return ctx.enter_context(nc.sbuf_tensor(name, shape, dt))

        def ps(name, shape):
            return ctx.enter_context(nc.psum_tensor(name, shape, F32))

        def sem(name):
            return ctx.enter_context(nc.semaphore(name))

        nat = [sb(f"nat{t}", [P, TILE]) for t in range(2)]
        at = [sb(f"at{g}", [P, GSZ]) for g in range(NG)]
        high = [sb(f"high{g}", [P, GSZ], F32R) for g in range(NG)]
        low = [sb(f"low{k}", [P, GSZ], F32R) for k in range(2)]
        dx_t = sb("dx_t", [P, NB * BLK])
        x1 = sb("x1", [P, NB * BLK])
        part = sb("part", [P, NB * BLK])
        wa_h = sb("wa_h", [P, BLK], F32R)
        wa_l = sb("wa_l", [P, BLK], F32R)
        wb_h = sb("wb_h", [P, BLK], F32R)
        wb_l = sb("wb_l", [P, BLK], F32R)
        xrow = sb("xrow", [P, BLK])
        trow = sb("trow", [P, BLK])
        p0 = sb("p0", [P, BLK])
        z = sb("z", [P, BLK])
        w0t = sb("w0t", [P, D])
        cheb = sb("cheb", [P, 3 * D])
        bias0 = sb("bias0", [P, D])
        bias1 = sb("bias1", [P, D])
        ident = sb("ident", [P, P])
        ident_r = sb("ident_r", [P, P], F32R)
        ones_r = sb("ones_r", [P, P], F32R)
        same_q = [sb(f"same_q{q}", [P, P]) for q in range(NQ)]
        zeros = sb("zeros", [P, P], BF16)
        up_sum = sb("up_sum", [P, 2 * STRIPS * NB])
        zero_s = sb("zero_s", [P, 2 * STRIPS])
        up1 = sb("up1", [P, 2 * STRIPS])
        dcol = sb("dcol", [P, NB * CH])
        deg = sb("deg", [P, CH])
        is0 = sb("is0", [P, CH])
        safe = sb("safe", [P, CH])
        root = sb("root", [P, CH])
        stats = sb("stats", [P, 6 * CH])
        mean_var = sb("mean_var", [P, 2 * CH])
        mean = sb("mean", [P, CH])
        shift = sb("shift", [P, CH])
        var = sb("var", [P, CH])
        rstd = sb("rstd", [P, CH])
        neg_half = sb("neg_half", [P, CH])

        acc_a = ps("acc_a", [P, 2, HALF])
        acc_b = ps("acc_b", [P, 2, HALF])
        s0 = ps("s0", [P, BLK])
        s1 = ps("s1", [P, BLK])

        const_in = sem("const_in")
        pool_const = sem("pool_const")
        dve_const = sem("dve_const")
        w0_turned = sem("w0_turned")
        tile_in = [sem(f"tile_in{h}") for h in range(2)]
        strips_in = [sem(f"strips_in{h}") for h in range(2)]
        strips_free = sem("strips_free")
        nat_free = [sem(f"nat_free{h}") for h in range(2)]
        turned = sem("turned")
        high_set = sem("high_set")
        low_dve = sem("low_dve")
        low_pool = sem("low_pool")
        used = sem("used")
        wa_high = sem("wa_high")
        wa_low = sem("wa_low")
        wb_high = sem("wb_high")
        wb_low = sem("wb_low")
        a_taken = [sem(f"a_taken{h}") for h in range(2)]
        b_taken = [sem(f"b_taken{h}") for h in range(2)]
        xrow_in = sem("xrow_in")
        xb_set = sem("xb_set")
        z_set = sem("z_set")
        up_zeroed = sem("up_zeroed")
        sums_set = sem("sums_set")
        low_taken = sem("low_taken")
        deg_ps = sem("deg_ps")
        safe_set = sem("safe_set")
        root_set = sem("root_set")
        d_set = sem("d_set")
        dx_set = sem("dx_set")
        p0_set = sem("p0_set")
        part_zero = sem("part_zero")
        z_ps = sem("z_ps")
        s0_read = sem("s0_read")
        stats_set = sem("stats_set")
        aggr_set = sem("aggr_set")
        mean_set = sem("mean_set")
        var_set = sem("var_set")
        rstd_set = sem("rstd_set")
        x1_set = sem("x1_set")
        t_ps = sem("t_ps")
        t_set = sem("t_set")
        rows_set = sem("rows_set")
        rows_ps = sem("rows_ps")
        p12_set = sem("p12_set")
        u_read = sem("u_read")
        t2_set = sem("t2_set")
        out_ps = sem("out_ps")
        y_set = sem("y_set")
        y_out = sem("y_out")
        steps1 = sem("steps1")
        own_wait = sem("own_wait")
        DVE_CONST = 4 + NQ + NQ + 2

        def alone(wait):
            wait.then_inc(own_wait, 1)

        def blockof(t, i):
            return t[:, bass.ds(i * BLK, BLK)]

        def halfof(t, i, h):
            return t[:, bass.ds(i * BLK + h * HALF, HALF)]

        def per_chunk(t):
            return t.rearrange("p (b d) -> p b d", b=CH)

        def over_features(t):
            return t.unsqueeze(2).broadcast_to([P, CH, D])

        def over_chunks(t):
            return t.unsqueeze(1).broadcast_to([P, CH, D])

        def packed(t, h):
            return t[:].rearrange("p (b a c) -> p a b c", b=CH, a=NQ)[:, 2 * h:2 * h + 2]

        def in_order(t):
            return t.rearrange("p (a b c) -> p a b c", a=2, b=CH)

        def node_rows(t, i, a):
            return t[bass.ds(i * BLK + a * COLS_Q, COLS_Q), :].rearrange("(b c) d -> c b d", c=Q)

        def wait(engine, semaphore, value):
            if not isinstance(value, int) or value > 0:
                engine.wait_ge(semaphore, value)

        TWO = ([low[0], low[1], low[0], low[1]], 2)
        FOUR = ([low[0], low[1], wb_h, wb_l], NG)
        FOUR_NEXT = (FOUR[0], 2)

        def strip_of(h, s):
            return x1[:, (h * STRIPS + s) * BLK:(h * STRIPS + s + 1) * BLK]

        block = ctx.enter_context(nc.Block())

        @block.sync
        def _(sp):
            sp.dma_start(z[:, 0:D], w0).then_inc(const_in, 16)
            sp.dma_start(cheb[:].rearrange("p (k o) -> p k o", k=3), w1.rearrange("k d o -> d k o")).then_inc(const_in, 16)
            sp.dma_start(bias0[:], b0.partition_broadcast(P)).then_inc(const_in, 16)
            sp.dma_start(bias1[:], b1.partition_broadcast(P)).then_inc(const_in, 16)

            def tile(t, i, j, q):
                if not isinstance(q, int) or q > 0:
                    alone(sp.wait_ge(nat_free[t], q))
                for a in range(NQ):
                    src = adj[bass.ds(i * BLK, BLK), bass.ds(j * BLK + a * COLS_Q + t * COLS_T, COLS_T)]
                    dst = nat[t][Q * a:Q * a + Q, :].rearrange("r (g c) -> r g c", g=2 * GR)
                    sp.dma_start(dst, src.rearrange("(g r) c -> r g c", r=Q)).then_inc(tile_in[t], 16)

            def square(i, j, q):
                for t in range(2):
                    tile(t, i, j, q)

            def strips(h, i, j, count):
                for s in range(STRIPS):
                    if not isinstance(count, int) or count > 0:
                        alone(sp.wait_ge(strips_free, 2 * STRIPS * (count - 1) + STRIPS * h + s + 1))
                    src = adj[bass.ds(i * BLK + h * HALF + s * P, P), bass.ds(j * BLK, BLK)]
                    sp.dma_start(strip_of(h, s), src).then_inc(strips_in[h], 16)

            def row_1(i, more=None, strips_left=False):
                if more is None:
                    with sp.Fori(0, i) as m:
                        for t in range(2):
                            tile(t, i, m, q_1(i, m))
                            strips(t, i, NB - 1 - m, NB * i + m)
                    if strips_left:
                        with sp.Fori(0, NB - 2 * i) as e:
                            for h in range(2):
                                strips(h, i, i + e, NB * i + i + e)
                else:
                    with sp.Fori(0, more) as m:
                        square(i, m, q_1(i, m))
                    with sp.Fori(0, NB - i) as m:
                        for t in range(2):
                            tile(t, i, i - 1 - m, q_1(i, more + m))
                            strips(t, i, NB - 1 - m, NB * i + m)
                alone(sp.wait_ge(dx_set, i))
                load_x(i)

            def load_x(i):
                for a in range(NQ):
                    dst = xrow[Q * a:Q * a + Q, :].rearrange("c (b d) -> c b d", b=CH)
                    sp.dma_start(dst, node_rows(x, i, a)).then_inc(xrow_in, 16)

            load_x(0)
            for h in range(2):
                strips(h, 0, 0, 0)
            with sp.Fori(1, NB) as j:
                for h in range(2):
                    strips(h, 0, j, j)
            row_1(1, strips_left=True)
            with sp.Fori(2, MID) as i:
                row_1(i, strips_left=True)
            row_1(MID)
            with sp.Fori(0, NB - MID - 1) as k:
                row_1(MID + 1 + k, 2 * k + 2)
            square(NB - 1, NB - 1, q_2(0, 0))
            sp.wait_ge(dx_set, NB)
            load_x(NB - 1)
            with sp.Fori(1, NB) as r:
                with sp.Fori(0, r + 1) as m:
                    square(NB - 1 - r, NB - 1 - m, q_2(r, m))
                alone(sp.wait_ge(z_set, r))
                load_x(NB - 1 - r)
            with sp.Fori(0, NB) as i:
                with sp.Fori(0, i + 1) as j:
                    square(i, j, q_3(i, j))

            def store(r):
                alone(sp.wait_ge(y_set, r + 1))
                for a in range(NQ):
                    src = z[Q * a:Q * a + Q, :].rearrange("c (b d) -> c b d", b=CH)
                    sp.dma_start(node_rows(out, NB - 1 - r, a), src).then_inc(y_out, 16)

            for r in range(2):
                for m in range(r + 1):
                    square(NB - 1 - r, NB - 1 - m, q_4(r, m))
            with sp.Fori(2, NB) as r:
                store(r - 2)
                with sp.Fori(0, r + 1) as m:
                    square(NB - 1 - r, NB - 1 - m, q_4(r, m))
            store(NB - 2)
            store(NB - 1)
            sp.wait_ge(y_out, 16 * NQ * NB)

        @block.gpsimd
        def _(pool):
            nc.gpsimd.memset(ident[:], 0.0).then_inc(pool_const, 1)
            nc.gpsimd.memset(neg_half[:], -0.5).then_inc(pool_const, 1)
            pool.wait_ge(pool_const, 2)
            nc.gpsimd.affine_select(out=ident[:], in_=ident[:], compare_op=ALU.not_equal, fill=1.0, base=0,
                                    pattern=[[-1, P]], channel_multiplier=1).then_inc(pool_const, 1)

            def power(dst, src, signal):
                nc.gpsimd.tensor_tensor(dst[:], src[:], neg_half[:], ALU.pow).then_inc(signal, 1)

            def low_group(q, h, g, lows):
                to, back = lows
                pool.wait_ge(high_set, 2 * NG * q + NG * h + g + 1)
                wait(pool, used, 2 * NG * q + NG * h + g + 1 - back)
                nc.gpsimd.tensor_tensor(to[g][:], at[g][:], high[g][:].bitcast(F32), ALU.subtract).then_inc(low_pool, 1)

            def low_half(w_h, w_l, src, row, half, w_high, w_low, blocks):
                alone(pool.wait_ge(w_high, 2 * blocks + half + 1))
                part_ = slice(half * HALF, (half + 1) * HALF)
                nc.gpsimd.tensor_tensor(w_l[:, part_], halfof(src, row, half), w_h[:, part_].bitcast(F32),
                                        ALU.subtract).then_inc(w_low, 1)

            def low_block(q, row, a=None, b=None, lows=TWO, late=None):
                for t in range(2):
                    if a is not None:
                        low_half(wa_h, wa_l, dx_t, row, t, wa_high, wa_low, a)
                    if b is not None:
                        low_half(wb_h, wb_l, x1, row, t, wb_high, wb_low, b)
                    low_group(q, t, 1, lows)
                    if late is not None:
                        late(t)
                    low_group(q, t, 3, lows)

            pool.wait_ge(safe_set, 1)
            power(root, safe, root_set)
            low_block(0, 0, a=0, lows=FOUR)

            def root_1(i):
                pool.wait_ge(safe_set, i + 1)
                power(root, safe, root_set)

            def row_1(i, more):
                low_block(q_1(i, 0), 0, a=a_1(i, 0), lows=FOUR, late=lambda t: root_1(i - 1) if t == 1 else None)
                with pool.Fori(1, more if more is not None else i) as j:
                    low_block(q_1(i, j), j, a=a_1(i, j), lows=FOUR)
                if more is not None:
                    with pool.Fori(0, NB - i) as m:
                        low_block(q_1(i, more + m), i - 1 - m, a=a_1(i, more + m), lows=FOUR)

            with pool.Fori(2, MID + 1) as i:
                row_1(i, None)
            with pool.Fori(0, NB - MID - 1) as k:
                row_1(MID + 1 + k, 2 * k + 2)
            root_1(NB - 1)

            def power_norm(rows):
                pool.wait_ge(mean_set, rows + 1)
                pool.wait_ge(var_set, rows + 1)
                power(rstd, var, root_set)
                pool.wait_ge(root_set, NB + rows + 1)
                nc.gpsimd.tensor_tensor(shift[:], mean[:], rstd[:], ALU.mult).then_inc(rstd_set, 1)

            def bias_x(r):
                pool.wait_ge(xrow_in, 16 * NQ * (NB + r + 1))
                nc.gpsimd.tensor_tensor(per_chunk(xrow[:]), per_chunk(xrow[:]), over_chunks(bias0[:]),
                                        ALU.add).then_inc(xb_set, 1)

            low_block(q_2(0, 0), NB - 1, a=a_2(0, 0))
            pool.wait_ge(const_in, 16 * 4)
            bias_x(0)
            power_norm(0)
            low_block(q_2(1, 0), NB - 1, a=a_2(1, 0), b=b_2(1, 0))
            low_block(q_2(1, 1), NB - 2, a=a_2(1, 1))
            with pool.Fori(2, NB) as r:
                low_block(q_2(r, 0), NB - 1, a=a_2(r, 0), b=b_2(r, 0), late=lambda t: bias_x(r - 1) if t == 0 else None)
                power_norm(r - 1)
                with pool.Fori(1, r) as m:
                    low_block(q_2(r, m), NB - 1 - m, a=a_2(r, m), b=b_2(r, m))
                low_block(q_2(r, r), NB - 1 - r, a=a_2(r, r))
            bias_x(NB - 1)
            power_norm(NB - 1)
            low_block(q_3(0, 0), 0, b=b_3(0, 0))
            low_block(q_3(1, 0), 0, a=a_3(1, 0), b=b_3(1, 0))
            low_block(q_3(1, 1), 1, b=b_3(1, 1))
            with pool.Fori(2, NB) as i:
                with pool.Fori(0, i) as j:
                    low_block(q_3(i, j), j, a=a_3(i, j), b=b_3(i, j))
                low_block(q_3(i, i), i, b=b_3(i, i))

            low_block(q_4(0, 0), NB - 1, a=a_4(0, 0), lows=FOUR_NEXT)

            with pool.Fori(1, NB) as r:
                low_block(q_4(r, 0), NB - 1, a=a_4(r, 0), lows=FOUR)
                power_norm(NB + r - 1)
                with pool.Fori(1, r + 1) as m:
                    low_block(q_4(r, m), NB - 1 - m, a=a_4(r, m), lows=FOUR)
            power_norm(2 * NB - 1)

        @block.scalar
        def _(act):
            def copy(dst, src):
                return nc.scalar.activation(dst, src, ACT.Copy)

            def high_group(q, h, g, first=False):
                act.wait_ge(turned, 2 * NG * q + NG * h + g + 1)
                if h == 1 or not first:
                    act.wait_ge(used, 2 * NG * q + NG * (h - 1) + g + 1)
                copy(high[g][:], at[g][:]).then_inc(high_set, 1)

            def high_half(w_h, src, row, t, w_high, last):
                if last is not None:
                    act.wait_ge(used, 2 * NG * last + NG * (t + 1))
                part_ = slice(t * HALF, (t + 1) * HALF)
                copy(w_h[:, part_], halfof(src, row, t)).then_inc(w_high, 1)

            def high_block(q, row, a=None, b=None, first=False, between=None, beside=None):
                for t in range(2):
                    if a is not None:
                        high_half(wa_h, dx_t, row, t, wa_high, a if a is not False else None)
                    if b is not None:
                        high_half(wb_h, x1, row, t, wb_high, b if b is not False else None)
                    for g in range(NG):
                        high_group(q, t, g, first)
                        if beside is not None:
                            beside(t, g)
                        if (t, g) == (0, 1) and between is not None:
                            between(0)
                            between(1)
                    act.sem_inc(nat_free[t], 1)

            ups = up_sum[:].rearrange("p (s j) -> p s j", j=NB)

            def strip(h, s, j, count):
                if s == 0:
                    act.wait_ge(strips_in[h], 16 * DMAS * (count + 1))
                summed = nc.scalar.activation(strip_of(h, s), strip_of(h, s), ACT.Copy,
                                              accum_out=ups[:, STRIPS * h + s, bass.ds(j, 1)])
                summed.then_inc(strips_free, 1)

            def strips(j, count):
                for h in range(2):
                    for s in range(STRIPS):
                        strip(h, s, j, count)

            def take_h(i, h):
                act.wait_ge(used, 2 * NG * q_1(i, 0) - 1 + h)
                copy(halfof(part, i - 1, h), acc_a[:, h]).then_inc(a_taken[h], 1)

            def row_1(i, more=None, strips_left=False):
                act.wait_ge(sums_set, i)
                copy(ups[:, :, bass.ds(i - 1, 1)], zero_s[:].unsqueeze(2)).then_inc(up_zeroed, 1)

                def block_1(place, j, beside=None, between=None):
                    high_block(q_1(i, place), j, a=q_1(i, place) - 1, beside=beside, between=between)

                def sums_beside(m):
                    return lambda t, g: strip(t, g, NB - 1 - m, NB * i + m)

                def before(h):
                    take_h(i, h)

                if isinstance(i, int) and i == 1:
                    act.wait_ge(dx_set, 1)
                    high_block(0, 0, a=False, first=True, beside=sums_beside(0))
                elif more is None:
                    block_1(0, 0, sums_beside(0), before)
                    with act.Fori(1, i) as m:
                        act.wait_ge(dx_set, m + 1)
                        block_1(m, m, sums_beside(m))
                else:
                    block_1(0, 0, None, before)
                    with act.Fori(1, more) as m:
                        block_1(m, m)
                    act.wait_ge(dx_set, i)
                    with act.Fori(0, NB - i) as m:
                        block_1(more + m, i - 1 - m, sums_beside(m))
                if strips_left:
                    with act.Fori(0, NB - 2 * i) as e:
                        strips(i + e, NB * i + i + e)
                with act.Fori(0, i):
                    for h in range(2):
                        act.sem_inc(strips_in[h], 16 * DMAS)
                    act.sem_inc(strips_free, 2 * STRIPS)

            act.wait_ge(dve_const, DVE_CONST)
            with act.Fori(0, NB) as j:
                strips(j, j)
            row_1(1, strips_left=True)
            with act.Fori(2, MID) as i:
                row_1(i, strips_left=True)
            row_1(MID)
            with act.Fori(0, NB - MID - 1) as k:
                row_1(MID + 1 + k, 2 * k + 2)
            for h in range(2):
                take_h(NB, h)

            def features(t, b):
                return t[:, b * P:(b + 1) * P]

            def scale(rows, dst, signal, part_):
                if part_ == 0:
                    act.wait_ge(rstd_set, rows + 1)
                for b in range(CH // 2 * part_, CH // 2 * (part_ + 1)):
                    scaled = nc.scalar.activation(dst(b), features(z, b), ACT.Identity, scale=rstd[:, b:b + 1],
                                                  bias=shift[:, b:b + 1])
                if part_ == 1:
                    scaled.then_inc(signal, 1)

            def norm_0(r, part_):
                scale(r, lambda b: x1[:, bass.ds((NB - 1 - r) * BLK + b * P, P)], x1_set, part_)

            def in_tile_0(norm, r):
                return lambda t, g: norm(r, g - 1) if t == 0 and g in (1, 2) else None

            def take_b(r, h):
                act.wait_ge(p0_set, 2 * r + h + 1)
                copy(halfof(part, NB - 1 - r, h), acc_b[:, h]).then_inc(b_taken[h], 1)

            act.wait_ge(dx_set, NB)
            high_block(q_2(0, 0), NB - 1, a=q_2(0, 0) - 1)
            norm_0(0, 0)
            norm_0(0, 1)
            act.wait_ge(x1_set, 1)
            high_block(q_2(1, 0), NB - 1, a=q_2(1, 0) - 1, b=False)
            high_block(q_2(1, 1), NB - 2, a=q_2(1, 1) - 1)

            def block_2(r, m, beside=None):
                high_block(q_2(r, m), NB - 1 - m, a=q_2(r, m) - 1, b=q_2(r, m) - 1, beside=beside)

            def block_20(r):
                high_block(q_2(r, 0), NB - 1, a=q_2(r, 0) - 1, b=q_2(r, 0) - 2, between=lambda h: take_b(r - 1, h))

            block_20(2)
            norm_0(1, 0)
            norm_0(1, 1)
            act.wait_ge(x1_set, 2)
            block_2(2, 1)
            high_block(q_2(2, 2), NB - 3, a=q_2(2, 2) - 1)
            with act.Fori(3, NB) as r:
                block_20(r)
                block_2(r, 1, beside=in_tile_0(norm_0, r - 1))
                with act.Fori(2, r) as m:
                    act.wait_ge(x1_set, m + 1)
                    block_2(r, m)
                high_block(q_2(r, r), NB - 1 - r, a=q_2(r, r) - 1)
            take_b(NB - 1, 0)
            take_b(NB - 1, 1)
            norm_0(NB - 1, 0)
            norm_0(NB - 1, 1)

            def take_t(i):
                act.wait_ge(t_ps, i + 1)
                copy(blockof(dx_t, i), s0[:]).then_inc(t_set, 1)
                act.wait_ge(t_set, i + 1)

            def take_u(i, h):
                act.wait_ge(p0_set, 2 * NB + 2 * i + h + 1)
                copy(halfof(part, i, h), acc_a[:, h]).then_inc(a_taken[h], 1)

            act.wait_ge(x1_set, NB)
            high_block(q_3(0, 0), 0, b=q_3(0, 0) - 2)
            take_t(0)
            high_block(q_3(1, 0), 0, a=q_3(1, 0) - 2, b=q_3(1, 0) - 1)
            high_block(q_3(1, 1), 1, b=q_3(1, 1) - 1)
            with act.Fori(2, NB) as i:
                high_block(q_3(i, 0), 0, a=q_3(i, 0) - 2, b=q_3(i, 0) - 1, between=lambda h: take_u(i - 1, h))
                take_t(i - 1)
                with act.Fori(1, i) as j:
                    high_block(q_3(i, j), j, a=q_3(i, j) - 1, b=q_3(i, j) - 1)
                high_block(q_3(i, i), i, b=q_3(i, i) - 1)
            take_u(NB - 1, 0)
            take_u(NB - 1, 1)
            take_t(NB - 1)

            def stage_rows(r):
                if not isinstance(r, int) or r > 0:
                    act.wait_ge(out_ps, r)
                copy(xrow[:], blockof(x1, NB - 1 - r)).then_inc(rows_set, 1)
                copy(trow[:], blockof(dx_t, NB - 1 - r)).then_inc(rows_set, 1)

            def take_rows(r):
                act.wait_ge(rows_ps, 2 * r + 1)
                copy(xrow[:], s0[:]).then_inc(p12_set, 1)
                act.wait_ge(rows_ps, 2 * r + 2)
                copy(trow[:], s1[:]).then_inc(p12_set, 1)

            def norm_1(r, part_):
                scale(NB + r, lambda b: features(z, b), y_set, part_)

            act.wait_ge(z_set, NB)
            high_block(q_4(0, 0), NB - 1, a=q_4(0, 0) - 2)
            stage_rows(0)
            take_rows(0)

            def row_4(r, longer):
                high_block(q_4(r, 0), NB - 1, a=q_4(r, 0) - 1)
                stage_rows(r)
                high_block(q_4(r, 1), NB - 2, a=q_4(r, 1) - 1, beside=in_tile_0(norm_1, r - 1))
                if longer:
                    with act.Fori(2, r + 1) as m:
                        high_block(q_4(r, m), NB - 1 - m, a=q_4(r, m) - 1)
                take_rows(r)

            row_4(1, False)
            with act.Fori(2, NB) as r:
                row_4(r, True)
            norm_1(NB - 1, 0)
            norm_1(NB - 1, 1)

        @block.vector
        def _(dve):
            nc.vector.memset(zero_s[:], 0.0).then_inc(dve_const, 1)
            nc.vector.memset(zeros[:], 0.0).then_inc(dve_const, 1)
            nc.vector.memset(ones_r[:].bitcast(F32), 1.0).then_inc(dve_const, 1)
            nc.vector.memset(blockof(part, 0), 0.0).then_inc(dve_const, 1)
            for q in range(NQ):
                nc.vector.memset(same_q[q][:], 0.0).then_inc(dve_const, 1)
            dve.wait_ge(pool_const, 3)
            dve.wait_ge(dve_const, 4 + NQ)
            for q in range(NQ):
                rows = slice(Q * q, Q * q + Q)
                corner = ident[rows, Q * q:Q * q + Q].unsqueeze(1).broadcast_to([Q, NQ, Q])
                nc.vector.tensor_copy(same_q[q][rows, :].rearrange("p (a c) -> p a c", a=NQ), corner).then_inc(dve_const, 1)
            nc.vector.tensor_copy(ident_r[:], ident[:]).then_inc(dve_const, 1)
            dve.wait_ge(w0_turned, 1)
            nc.vector.tensor_copy(w0t[:], s1[:, 0:D]).then_inc(dve_const, 1)

            def own_order(signal, start):
                count = [0]

                def step(ins):
                    count[0] += 1
                    ins.then_inc(signal, 1)
                    dve.wait_ge(signal, start + count[0])
                return step

            def turn(q, h, g, first=False):
                if h == 1 or not first:
                    if g % 2:
                        dve.wait_ge(low_pool, NG * q + NG // 2 * (h - 1) + g // 2 + 1)
                    else:
                        dve.wait_ge(low_dve, NG * q + NG // 2 * (h - 1) + g // 2 + 1)
                half, pair = g % 2, g // 2
                src = nat[h][:].rearrange("p (g b c) -> p g b c", g=2 * GR, b=CH // 2)
                src = src[:, GR * half:GR * (half + 1), GC * pair:GC * (pair + 1)]
                dst = at[g][:].rearrange("p (b g r) -> p g b r", b=GC, g=GR)
                nc.vector.transpose(dst, src).then_inc(turned, 1)

            def low_group(q, h, g, lows):
                to, back = lows
                dve.wait_ge(high_set, 2 * NG * q + NG * h + g + 1)
                wait(dve, used, 2 * NG * q + NG * h + g + 1 - back)
                nc.vector.tensor_tensor(to[g][:], at[g][:], high[g][:].bitcast(F32), ALU.subtract).then_inc(low_dve, 1)

            def tile(q, h, first=False, between=None, late=None, after=None, lows=TWO):
                dve.wait_ge(tile_in[h], 16 * DMAS * (q + 1))
                for g in range(0, NG, 2):
                    turn(q, h, g, first)
                    turn(q, h, g + 1, first)
                    if g == 0 and between is not None:
                        between(0)
                    if g > 0 and late is not None:
                        late()
                    low_group(q, h, g, lows)
                    if g == 0 and between is not None:
                        between(1)
                if after is not None:
                    after()

            def both(q, first=False, between=None, late=None, after=None, lows=TWO):
                tile(q, 0, first, between, lows=lows)
                tile(q, 1, first, late=late, after=after, lows=lows)

            STEPS1 = NQ + 3

            def sums_up(i):
                dve.wait_ge(strips_free, 2 * STRIPS * (NB * i + NB))
                if not isinstance(i, int) or i > 0:
                    dve.wait_ge(up_zeroed, i)
                nc.vector.tensor_reduce(up1[:], ups, AX_X, ALU.add).then_inc(sums_set, 1)

            def sums_half(i, h):
                if h == 0:
                    sums_up(i - 1)
                    if not isinstance(i, int) or i > 2:
                        dve.wait_ge(deg_ps, i - 1)
                dve.wait_ge(used, 2 * NG * q_1(i, 0) - 1 + h)
                nc.vector.tensor_copy(packed(p0, h), in_order(acc_b[:, h])).then_inc(low_taken, 1)

            def degree(i):
                step = own_order(steps1, STEPS1 * i)
                dve.wait_ge(deg_ps, i + 1)
                for a in range(NQ):
                    rows = slice(Q * a, Q * a + Q)
                    step(nc.vector.tensor_scalar(deg[rows, :], s1[rows, CH * a:CH * a + CH], 1.0, None, ALU.add))
                if not isinstance(i, int) or i > 0:
                    step(nc.vector.tensor_tensor(deg[:], deg[:], s1[:, 2 * GR:2 * GR + CH], ALU.add))
                else:
                    step(nc.vector.tensor_scalar(deg[:], deg[:], 0.0, None, ALU.add))
                step(nc.vector.tensor_scalar(is0[:], deg[:], 0.0, None, ALU.is_equal))
                nc.vector.tensor_tensor(safe[:], deg[:], is0[:], ALU.add).then_inc(safe_set, 1)

            def dx(i):
                step = own_order(steps1, STEPS1 * i + NQ + 2)
                dve.wait_ge(safe_set, i + 1)
                step(nc.vector.tensor_scalar(is0[:], is0[:], -1.0, 1.0, ALU.mult, ALU.add))
                dve.wait_ge(root_set, i + 1)
                d_i = dcol[:, bass.ds(i * CH, CH)]
                nc.vector.tensor_tensor(d_i, root[:], is0[:], ALU.mult).then_inc(d_set, 1)
                dve.wait_ge(d_set, i + 1)
                dve.wait_ge(xrow_in, 16 * NQ * (i + 1))
                nc.vector.tensor_tensor(per_chunk(blockof(dx_t, i)), per_chunk(xrow[:]), over_features(d_i),
                                        ALU.mult).then_inc(dx_set, 1)

            ups = up_sum[:].rearrange("p (s j) -> p s j", j=NB)
            sums_up(0)
            degree(0)
            dx(0)
            both(0, first=True, lows=FOUR)
            with dve.Fori(2, NB) as i:
                both(q_1(i, 0), between=lambda h: sums_half(i, h), late=lambda: degree(i - 1), after=lambda: dx(i - 1),
                     lows=FOUR)
                with dve.Fori(1, i) as j:
                    both(q_1(i, j), lows=FOUR)
            for h in range(2):
                sums_half(NB, h)
            degree(NB - 1)
            dx(NB - 1)

            def moments(rows):
                for b in range(CH):
                    stat = nc.vector.bn_stats(out=stats[:, 6 * b:6 * b + 6], in_=z[:, b * P:(b + 1) * P])
                stat.then_inc(stats_set, 1)
                alone(dve.wait_ge(stats_set, rows + 1))
                for b in range(CH):
                    stat = nc.vector.bn_aggr(out=mean_var[:, 2 * b:2 * b + 2], in_=stats[:, 6 * b:6 * b + 6])
                stat.then_inc(aggr_set, 1)
                dve.wait_ge(aggr_set, rows + 1)
                both_ = mean_var[:].rearrange("p (b k) -> p k b", k=2)
                nc.vector.tensor_scalar(mean[:], both_[:, 0], -1.0, None, ALU.mult).then_inc(mean_set, 1)
                nc.vector.tensor_scalar(var[:], both_[:, 1], LN_EPS, None, ALU.add).then_inc(var_set, 1)

            def h_half(r, h):
                alone(dve.wait_ge(used, 2 * NG * q_2(r, r) + 2 * NG - 1 + h))
                nc.vector.tensor_tensor(packed(p0, h), in_order(acc_a[:, h]), in_order(halfof(part, NB - 1 - r, h)),
                                        ALU.add).then_inc(p0_set, 1)

            def z_0(r):
                i = NB - 1 - r
                dve.wait_ge(z_ps, r + 1)
                if not isinstance(r, int) or r > 0:
                    dve.wait_ge(x1_set, r)
                nc.vector.tensor_tensor(per_chunk(z[:]), per_chunk(s0[:]), over_features(dcol[:, bass.ds(i * CH, CH)]),
                                        ALU.mult).then_inc(s0_read, 1)
                dve.wait_ge(s0_read, r + 1)
                dve.wait_ge(xb_set, r + 1)
                nc.vector.tensor_tensor(z[:], z[:], xrow[:], ALU.add).then_inc(z_set, 1)
                dve.wait_ge(z_set, r + 1)
                moments(r)

            for h in range(2):
                dve.wait_ge(a_taken[h], NB - 1)
            both(q_2(0, 0))
            h_half(0, 0)
            h_half(0, 1)
            dve.wait_ge(p0_set, 2)
            nc.vector.memset(blockof(part, NB - 1), 0.0).then_inc(part_zero, 1)
            z_0(0)
            both(q_2(1, 0))
            both(q_2(1, 1))
            with dve.Fori(2, NB) as r:
                both(q_2(r, 0), between=lambda h: h_half(r - 1, h), late=lambda: z_0(r - 1))
                with dve.Fori(1, r + 1) as m:
                    both(q_2(r, m))
            h_half(NB - 1, 0)
            h_half(NB - 1, 1)
            z_0(NB - 1)

            def t_half(i, h):
                if not isinstance(i, int) or i > 0:
                    dve.wait_ge(t_ps, i)
                alone(dve.wait_ge(used, 2 * NG * q_3(i, i) + 2 * NG - 1 + h))
                nc.vector.tensor_tensor(packed(p0, h), in_order(acc_b[:, h]), in_order(halfof(part, i, h)),
                                        ALU.add).then_inc(p0_set, 1)

            dve.wait_ge(part_zero, 1)
            for h in range(2):
                dve.wait_ge(b_taken[h], NB - 1)
            both(q_3(0, 0))
            t_half(0, 0)
            t_half(0, 1)
            dve.wait_ge(p0_set, 2 * NB + 2)
            nc.vector.memset(blockof(part, 0), 0.0).then_inc(part_zero, 1)
            both(q_3(1, 0))
            both(q_3(1, 1))
            with dve.Fori(2, NB) as i:
                both(q_3(i, 0), between=lambda h: t_half(i - 1, h))
                with dve.Fori(1, i + 1) as j:
                    both(q_3(i, j))
            t_half(NB - 1, 0)
            t_half(NB - 1, 1)

            def u_half(r, h):
                alone(dve.wait_ge(used, 2 * NG * q_4(r, r) + 2 * NG - 1 + h))
                nc.vector.tensor_tensor(packed(p0, h), in_order(acc_a[:, h]), in_order(halfof(part, NB - 1 - r, h)),
                                        ALU.add).then_inc(u_read, 1)

            def t2(r):
                dve.wait_ge(u_read, 2 * r + 2)
                dve.wait_ge(p12_set, 2 * r + 1)
                nc.vector.scalar_tensor_tensor(out=p0[:], in0=p0[:], scalar=2.0, in1=xrow[:], op0=ALU.mult,
                                               op1=ALU.subtract).then_inc(t2_set, 1)

            def z_1(r):
                dve.wait_ge(out_ps, r + 1)
                if isinstance(r, int) and r == 0:
                    dve.wait_ge(x1_set, NB)
                else:
                    dve.wait_ge(y_out, 16 * NQ * r)
                nc.vector.tensor_tensor(z[:], s0[:], blockof(x1, NB - 1 - r), ALU.add).then_inc(s0_read, 1)
                dve.wait_ge(s0_read, NB + r + 1)
                moments(NB + r)

            dve.wait_ge(t_ps, NB)
            dve.wait_ge(part_zero, 2)
            for h in range(2):
                dve.wait_ge(a_taken[h], 2 * NB - 2)
            both(q_4(0, 0), lows=FOUR_NEXT)

            def row_4(r):
                tile(q_4(r, 0), 0, between=lambda h: u_half(r - 1, h), lows=FOUR)
                t2(r - 1)
                tile(q_4(r, 0), 1, late=lambda: z_1(r - 1), lows=FOUR)
                with dve.Fori(1, r + 1) as m:
                    both(q_4(r, m), lows=FOUR)

            row_4(1)
            with dve.Fori(2, NB) as r:
                row_4(r)
            u_half(NB - 1, 0)
            u_half(NB - 1, 1)
            t2(NB - 1)
            z_1(NB - 1)

        @block.tensor
        def _(pe):
            def chunk(t, b):
                return t[:, b * P:(b + 1) * P]

            def clear(acc, h):
                for b in range(HALF // P):
                    pe.matmul(acc[:, h, b * P:(b + 1) * P], zeros[:], zeros[:], start=(b == 0), stop=False,
                              skip_group_check=True)

            def add(to, w, m, stop=False):
                return pe.matmul(to, w, m, start=False, stop=stop, skip_group_check=True)

            def tile(q, t, a=None, b=None, sums=False, diagonal=False, opening=None, lows=TWO):
                for g in range(NG):
                    h, pair = g % 2, g // 2
                    if g < 2 and opening is not None:
                        opening(h)
                    pe.wait_ge(high_set, 2 * NG * q + NG * t + g + 1)
                    products = [(acc_b, wb_h, wb_l, wb_low, b), (acc_a, wa_h, wa_l, wa_low, a)]
                    products = [p for p in products if p[-1] is not None]
                    for acc, w_h, w_l, w_low, blocks in products:
                        if g == 0:
                            pe.wait_ge(w_low, 2 * blocks + t + 1)
                        for c in range(GC):
                            ch = CH // 2 * t + GC * pair + c
                            cols = slice(c * HALF, (c + 1) * HALF)
                            if diagonal:
                                to = acc[:, h].rearrange("p (a b c) -> p a b c", a=2, b=CH)[:, :, ch]
                                eye = ident_r[:, 2 * Q * h:2 * Q * (h + 1)].rearrange("p (a c) -> p a c", a=2)
                                add(to, chunk(w_h, ch), eye)
                                add(to, chunk(w_l, ch), eye)
                            add(acc[:, h], chunk(w_h, ch), high[g][:, cols])
                            add(acc[:, h], chunk(w_l, ch), high[g][:, cols])
                    if sums:
                        for c in range(GC):
                            add(acc_b[:, h], ones_r[:], high[g][:, c * HALF:(c + 1) * HALF])
                    pe.wait_ge(low_pool if g % 2 else low_dve, NG * q + NG // 2 * t + g // 2 + 1)
                    for c in range(GC):
                        cols = slice(c * HALF, (c + 1) * HALF)
                        for acc, w_h, w_l, w_low, blocks in products:
                            last = add(acc[:, h], chunk(w_h, CH // 2 * t + GC * pair + c), lows[0][g][:, cols], stop=True)
                        if sums:
                            last = add(acc_b[:, h], ones_r[:], lows[0][g][:, cols], stop=True)
                    last.then_inc(used, 1)

            pe.wait_ge(const_in, 16 * 4)
            pe.wait_ge(pool_const, 3)
            pe.transpose(s1[:, 0:D], z[:, 0:D], ident[:]).then_inc(w0_turned, 1)
            pe.wait_ge(dve_const, DVE_CONST)

            def degrees(i):
                pe.wait_ge(sums_set, i + 1)
                for q in range(NQ):
                    to = s1[:, 0:2 * GR].rearrange("p (s q) -> p q s", q=NQ)[:, q]
                    mm = pe.matmul(to, same_q[q][:], up1[:], start=(q == 0), stop=(q == NQ - 1), skip_group_check=True)
                if not isinstance(i, int) or i > 0:
                    pe.wait_ge(low_taken, 2 * i)
                    for b in range(CH):
                        mm = add(s1[:, 2 * GR + b:2 * GR + b + 1], chunk(p0, b), ident[:, 0:1], stop=True)
                mm.then_inc(deg_ps, 1)

            degrees(0)
            for h in range(2):
                clear(acc_a, h)
                clear(acc_b, h)
            for t in range(2):
                tile(0, t, a=0, sums=True, lows=FOUR)
            with pe.Fori(2, NB) as i:
                def opening(h):
                    pe.wait_ge(a_taken[h], i - 1)
                    clear(acc_a, h)
                    pe.wait_ge(low_taken, 2 * i - 3 + h)
                    clear(acc_b, h)

                tile(q_1(i, 0), 0, a=a_1(i, 0), sums=True, opening=opening, lows=FOUR)
                degrees(i - 1)
                tile(q_1(i, 0), 1, a=a_1(i, 0), sums=True, lows=FOUR)
                with pe.Fori(1, i) as j:
                    for t in range(2):
                        tile(q_1(i, j), t, a=a_1(i, j), sums=True, lows=FOUR)
            degrees(NB - 1)

            def z_row(r):
                pe.wait_ge(p0_set, 2 * r + 2)
                if not isinstance(r, int) or r > 0:
                    pe.wait_ge(s0_read, r)
                for b in range(CH):
                    mm = pe.matmul(chunk(s0, b), chunk(p0, b), w0t[:], start=True, stop=True, skip_group_check=True)
                mm.then_inc(z_ps, 1)

            for h in range(2):
                pe.wait_ge(a_taken[h], NB - 1)
                clear(acc_a, h)
            for t in range(2):
                tile(q_2(0, 0), t, a=a_2(0, 0), diagonal=True)
            z_row(0)
            for h in range(2):
                clear(acc_a, h)
                pe.wait_ge(low_taken, 2 * NB - 2)
                clear(acc_b, h)
            for t in range(2):
                tile(q_2(1, 0), t, a=a_2(1, 0), b=b_2(1, 0))
            for t in range(2):
                tile(q_2(1, 1), t, a=a_2(1, 1), diagonal=True)
            with pe.Fori(2, NB) as r:
                def opening(h):
                    pe.wait_ge(p0_set, 2 * r - 1 + h)
                    clear(acc_a, h)
                    pe.wait_ge(b_taken[h], r - 1)
                    clear(acc_b, h)

                tile(q_2(r, 0), 0, a=a_2(r, 0), b=b_2(r, 0), opening=opening)
                z_row(r - 1)
                tile(q_2(r, 0), 1, a=a_2(r, 0), b=b_2(r, 0))
                with pe.Fori(1, r) as m:
                    for t in range(2):
                        tile(q_2(r, m), t, a=a_2(r, m), b=b_2(r, m))
                for t in range(2):
                    tile(q_2(r, r), t, a=a_2(r, r), diagonal=True)
            z_row(NB - 1)

            def t_row(i):
                pe.wait_ge(p0_set, 2 * NB + 2 * i + 2)
                if isinstance(i, int) and i == 0:
                    pe.wait_ge(s0_read, NB)
                else:
                    pe.wait_ge(t_set, i)
                for b in range(CH):
                    mm = pe.transpose(chunk(s0, b), chunk(p0, b), ident[:])
                mm.then_inc(t_ps, 1)

            for h in range(2):
                pe.wait_ge(b_taken[h], NB - 1)
                clear(acc_b, h)
            for t in range(2):
                tile(q_3(0, 0), t, b=b_3(0, 0))
            t_row(0)
            for h in range(2):
                clear(acc_b, h)
                clear(acc_a, h)
            for t in range(2):
                tile(q_3(1, 0), t, a=a_3(1, 0), b=b_3(1, 0))
            for t in range(2):
                tile(q_3(1, 1), t, b=b_3(1, 1))
            with pe.Fori(2, NB) as i:
                def opening(h):
                    pe.wait_ge(p0_set, 2 * NB + 2 * i - 1 + h)
                    clear(acc_b, h)
                    pe.wait_ge(a_taken[h], NB - 1 + i - 1)
                    clear(acc_a, h)

                tile(q_3(i, 0), 0, a=a_3(i, 0), b=b_3(i, 0), opening=opening)
                t_row(i - 1)
                tile(q_3(i, 0), 1, a=a_3(i, 0), b=b_3(i, 0))
                with pe.Fori(1, i) as j:
                    for t in range(2):
                        tile(q_3(i, j), t, a=a_3(i, j), b=b_3(i, j))
                for t in range(2):
                    tile(q_3(i, i), t, b=b_3(i, i))
            t_row(NB - 1)

            def rows_back(r):
                pe.wait_ge(s0_read, NB + r)
                pe.wait_ge(rows_set, 2 * r + 2)
                for b in range(CH):
                    mm = pe.transpose(chunk(s0, b), chunk(xrow, b), ident[:])
                mm.then_inc(rows_ps, 1)
                for b in range(CH):
                    mm = pe.transpose(chunk(s1, b), chunk(trow, b), ident[:])
                mm.then_inc(rows_ps, 1)

            def out_row(r):
                pe.wait_ge(p12_set, 2 * r + 2)
                pe.wait_ge(t2_set, r + 1)
                for b in range(CH):
                    pe.matmul(chunk(s0, b), ones_r[0:1, :].bitcast(F32), bias1[0:1, :], start=True, stop=False,
                              skip_group_check=True)
                    for n, src in enumerate((xrow, trow, p0)):
                        mm = add(chunk(s0, b), chunk(src, b), cheb[:, n * D:(n + 1) * D], stop=(n == 2))
                mm.then_inc(out_ps, 1)

            for h in range(2):
                pe.wait_ge(a_taken[h], 2 * NB - 2)
                clear(acc_a, h)
            for t in range(2):
                tile(q_4(0, 0), t, a=a_4(0, 0), lows=FOUR)
            pe.wait_ge(t_set, NB)
            rows_back(0)
            with pe.Fori(1, NB) as r:
                def opening(h):
                    pe.wait_ge(u_read, 2 * r - 1 + h)
                    clear(acc_a, h)

                tile(q_4(r, 0), 0, a=a_4(r, 0), opening=opening, lows=FOUR)
                out_row(r - 1)
                tile(q_4(r, 0), 1, a=a_4(r, 0), lows=FOUR)
                rows_back(r)
                with pe.Fori(1, r + 1) as m:
                    for t in range(2):
                        tile(q_4(r, m), t, a=a_4(r, m), lows=FOUR)
            out_row(NB - 1)


_INPUTS = ["x", "adj", "L0_gnn_W", "L0_gnn_b", "L1_gnn_weight", "L1_gnn_bias"]


def kernel(**inputs):
    import numpy as np
    import concourse.bacc as bacc
    from concourse.bass_utils import run_bass_kernel_spmd

    nc = bacc.Bacc("TRN2", target_bir_lowering=False, num_devices=1)
    arrays, args = {}, []
    for name in _INPUTS:
        a = np.ascontiguousarray(inputs[name])
        arrays[f"in_{name}"] = a
        args.append(nc.dram_tensor(f"in_{name}", a.shape, mybir.dt.from_np(a.dtype), kind="ExternalInput").ap())
    out = nc.dram_tensor("out_rows", arrays["in_x"].shape, F32, kind="ExternalOutput").ap()
    build(nc, *args, out)
    return run_bass_kernel_spmd(nc, [arrays], core_ids=[0]).results[0]["out_rows"]
```
